# Optimizing a Trainium2 kernel written in Bass

```python
import numpy as np
import jax
import jax.numpy as jnp

def _softmax(x, axis=-1):
    return jax.nn.softmax(x, axis=axis)

def _gelu(x):
    return jax.nn.gelu(x, approximate=True)

def _silu(x):
    return jax.nn.silu(x)

def _sigmoid(x):
    return jax.nn.sigmoid(x)

def _layernorm(x, axis=-1, eps=1e-05):
    m = jnp.mean(x, axis=axis, keepdims=True)
    v = jnp.var(x, axis=axis, keepdims=True)
    return (x - m) / jnp.sqrt(v + eps)

def _scatter_add(tgt, idx, src, axis=0):
    return tgt.at[idx].add(src)

def _segment_sum(src, seg, n):
    return jax.ops.segment_sum(src, seg, n)
kernel_name = 'mk_prb_d1_jaxref_r8_8dfbfc'

def setup_inputs(seed: int=0):
    np.random.seed(seed)
    _w = jnp.asarray

    def _L0_attn_setup():
        import jax, jax.numpy as jnp
        import numpy as np
        DIM = 256
        HEAD_DIM = 64
        D_H = 64
        ATTN_HEAD_DIM = 128
        NH = DIM // HEAD_DIM
        NAH = DIM // ATTN_HEAD_DIM
        BATCH, SEQ = (1, 512)
        CHUNK = 128
        WINDOW = 128
        BASE_LR = 0.01
        BASE_LR_INV = float(BASE_LR + np.log(-np.expm1(-BASE_LR)))
        NS_COEFFS = [(4.0848, -6.8946, 2.927), (3.9505, -6.3029, 2.6377), (3.7418, -5.5913, 2.3037), (2.8769, -3.1427, 1.2046), (2.8366, -3.0525, 1.2012)]

        def _silu_bp(dy, x):
            s = jax.nn.sigmoid(x)
            return dy * s * (1 + x * (1 - s))

        def _l2norm(t):
            return t / (jnp.linalg.norm(t, axis=-1, keepdims=True) + 1e-05)

        def _newtonschulz5(G):
            X = G
            tr = G.shape[1] > G.shape[2]
            if tr:
                X = X.transpose(0, 2, 1)
            X = X / (jnp.sqrt(jnp.sum(X * X, axis=(1, 2), keepdims=True)) + 1e-07)
            for a, b, c in NS_COEFFS:
                A = X @ X.transpose(0, 2, 1)
                B = b * A + c * (A @ A)
                X = a * X + B @ X
            if tr:
                X = X.transpose(0, 2, 1)
            return X
        key = jax.random.key(seed)
        ks = jax.random.split(key, 12)
        f32 = jnp.float32
        return {'x': jax.random.normal(ks[0], (BATCH, SEQ, DIM), f32), 'Wqkv': jax.random.normal(ks[1], (DIM, 3 * DIM), f32) / np.sqrt(DIM), 'Wlr': jax.random.normal(ks[2], (DIM, 3 * NH), f32) / np.sqrt(DIM), 'Wm': jax.random.normal(ks[3], (DIM, NH), f32) / np.sqrt(DIM), 'bm': jnp.zeros((NH,), f32), 'Ws': jax.random.normal(ks[4], (DIM, NH), f32) / np.sqrt(DIM), 'bs': jnp.zeros((NH,), f32), 'Wo': jax.random.normal(ks[5], (DIM, DIM), f32) / np.sqrt(DIM), 'w0': jax.random.normal(ks[6], (NH, D_H, HEAD_DIM), f32) / np.sqrt(HEAD_DIM), 'w1': jax.random.normal(ks[7], (NH, HEAD_DIM, D_H), f32) / np.sqrt(D_H), 'w2': jax.random.normal(ks[8], (NH, D_H, HEAD_DIM), f32) / np.sqrt(HEAD_DIM), 'o_norm_g': jnp.ones((HEAD_DIM,), f32), 'qk_scale': jnp.ones((DIM, 2), f32), 'qk_offset': jnp.zeros((DIM, 2), f32)}
    _L0_attn_in = _L0_attn_setup()

    def _L0_ffn_setup():
        import jax, jax.numpy as jnp
        import numpy as np
        H, LAT, INTER, E, G, TOPK_G, TOP_K = (256, 128, 128, 32, 4, 2, 8)
        SHARED_INTER = 512
        ROUTED_SCALE = 2.5
        B, S = (2, 128)

        def relu2(x):
            return jnp.square(jax.nn.relu(x))
        key = jax.random.key(seed)
        ks = jax.random.split(key, 9)
        w = 0.02
        return {'hidden_states': jax.random.normal(ks[0], (B, S, H), jnp.float32), 'gate_w': jax.random.normal(ks[1], (E, H), jnp.float32) * w, 'gate_bias': jax.random.normal(ks[2], (E,), jnp.float32) * w, 'fc1_w': jax.random.normal(ks[3], (LAT, H), jnp.float32) * w, 'fc2_w': jax.random.normal(ks[4], (H, LAT), jnp.float32) * w, 'w1': jax.random.normal(ks[5], (E, INTER, LAT), jnp.float32) * w, 'w2': jax.random.normal(ks[6], (E, LAT, INTER), jnp.float32) * w, 'shared_up_w': jax.random.normal(ks[7], (SHARED_INTER, H), jnp.float32) * w, 'shared_down_w': jax.random.normal(ks[8], (H, SHARED_INTER), jnp.float32) * w}
    _L0_ffn_in = _L0_ffn_setup()
    _d = {'L0_attn_x': _L0_attn_in['x'], 'L0_attn_Wqkv': _L0_attn_in['Wqkv'], 'L0_attn_Wlr': _L0_attn_in['Wlr'], 'L0_attn_Wm': _L0_attn_in['Wm'], 'L0_attn_bm': _L0_attn_in['bm'], 'L0_attn_Ws': _L0_attn_in['Ws'], 'L0_attn_bs': _L0_attn_in['bs'], 'L0_attn_Wo': _L0_attn_in['Wo'], 'L0_attn_w0': _L0_attn_in['w0'], 'L0_attn_w1': _L0_attn_in['w1'], 'L0_attn_w2': _L0_attn_in['w2'], 'L0_attn_o_norm_g': _L0_attn_in['o_norm_g'], 'L0_attn_qk_scale': _L0_attn_in['qk_scale'], 'L0_attn_qk_offset': _L0_attn_in['qk_offset'], 'L0_ffn_gate_w': _L0_ffn_in['gate_w'], 'L0_ffn_gate_bias': _L0_ffn_in['gate_bias'], 'L0_ffn_fc1_w': _L0_ffn_in['fc1_w'], 'L0_ffn_fc2_w': _L0_ffn_in['fc2_w'], 'L0_ffn_w1': _L0_ffn_in['w1'], 'L0_ffn_w2': _L0_ffn_in['w2'], 'L0_ffn_shared_up_w': _L0_ffn_in['shared_up_w'], 'L0_ffn_shared_down_w': _L0_ffn_in['shared_down_w']}
    _x0 = _d['L0_attn_x']
    _d['L0_attn_x'] = jax.random.normal(jax.random.fold_in(jax.random.key(seed), 1), (1, 2048, 256), dtype=_x0.dtype)
    del _x0
    return _d

def reference(L0_attn_x, L0_attn_Wqkv, L0_attn_Wlr, L0_attn_Wm, L0_attn_bm, L0_attn_Ws, L0_attn_bs, L0_attn_Wo, L0_attn_w0, L0_attn_w1, L0_attn_w2, L0_attn_o_norm_g, L0_attn_qk_scale, L0_attn_qk_offset, L0_ffn_gate_w, L0_ffn_gate_bias, L0_ffn_fc1_w, L0_ffn_fc2_w, L0_ffn_w1, L0_ffn_w2, L0_ffn_shared_up_w, L0_ffn_shared_down_w):

    def _L0_attn_ref(x, Wqkv, Wlr, Wm, bm, Ws, bs, Wo, w0, w1, w2, o_norm_g, qk_scale, qk_offset):
        import jax, jax.numpy as jnp
        import numpy as np
        DIM = 256
        HEAD_DIM = 64
        D_H = 64
        ATTN_HEAD_DIM = 128
        NH = DIM // HEAD_DIM
        NAH = DIM // ATTN_HEAD_DIM
        BATCH, SEQ = (1, 512)
        CHUNK = 128
        WINDOW = 128
        BASE_LR = 0.01
        BASE_LR_INV = float(BASE_LR + np.log(-np.expm1(-BASE_LR)))
        NS_COEFFS = [(4.0848, -6.8946, 2.927), (3.9505, -6.3029, 2.6377), (3.7418, -5.5913, 2.3037), (2.8769, -3.1427, 1.2046), (2.8366, -3.0525, 1.2012)]

        def _silu_bp(dy, x):
            s = jax.nn.sigmoid(x)
            return dy * s * (1 + x * (1 - s))

        def _l2norm(t):
            return t / (jnp.linalg.norm(t, axis=-1, keepdims=True) + 1e-05)

        def _newtonschulz5(G):
            X = G
            tr = G.shape[1] > G.shape[2]
            if tr:
                X = X.transpose(0, 2, 1)
            X = X / (jnp.sqrt(jnp.sum(X * X, axis=(1, 2), keepdims=True)) + 1e-07)
            for a, b, c in NS_COEFFS:
                A = X @ X.transpose(0, 2, 1)
                B = b * A + c * (A @ A)
                X = a * X + B @ X
            if tr:
                X = X.transpose(0, 2, 1)
            return X
        b, L, d = x.shape
        attn_qkv = x @ Wqkv
        ttt = jax.nn.silu(attn_qkv).reshape(b, L, 3, NH, HEAD_DIM)

        def heads(t):
            return t.transpose(0, 2, 1, 3).reshape(b * NH, L, HEAD_DIM)
        q = _l2norm(heads(ttt[:, :, 0]))
        k = _l2norm(heads(ttt[:, :, 1]))
        v = heads(ttt[:, :, 2])
        lr = jax.nn.softplus(x @ Wlr + BASE_LR_INV).reshape(b, L, NH, 3, 1)

        def lr_h(i):
            return lr[:, :, :, i, :].transpose(0, 2, 1, 3).reshape(b * NH, L, 1)
        lr0, lr1, lr2 = (lr_h(0), lr_h(1), lr_h(2))
        mom = jax.nn.sigmoid(x @ Wm + bm).reshape(b, L, NH, 1)
        mom = mom.transpose(0, 2, 1, 3).reshape(b * NH, L, 1)
        w0b = jnp.tile(w0, (b, 1, 1))
        w1b = jnp.tile(w1, (b, 1, 1))
        w2b = jnp.tile(w2, (b, 1, 1))
        n0 = jnp.linalg.norm(w0b, axis=2, keepdims=True)
        n1 = jnp.linalg.norm(w1b, axis=2, keepdims=True)
        n2 = jnp.linalg.norm(w2b, axis=2, keepdims=True)
        nc = L // CHUNK

        def chunkit(t):
            return t.reshape(b * NH, nc, CHUNK, -1).transpose(1, 0, 2, 3)
        xs = tuple(map(chunkit, (q, k, v, lr0, lr1, lr2, mom)))

        def step(carry, xi):
            W0, W1, W2, M0, M1, M2 = carry
            qi, ki, vi, l0, l1, l2, mi = xi
            hid = jnp.einsum('bcd,bhd->bch', qi, W2)
            gate = jax.nn.silu(jnp.einsum('bcd,bhd->bch', qi, W0))
            out = jnp.einsum('bch,boh->bco', gate * hid, W1)
            gba = jnp.einsum('bcd,bhd->bch', ki, W0)
            hbm = jnp.einsum('bcd,bhd->bch', ki, W2)
            sg = jax.nn.silu(gba)
            hidden = sg * hbm
            dhidden = jnp.einsum('bco,boh->bch', vi, W1)
            dhbm = dhidden * sg
            dgba = _silu_bp(dhidden * hbm, gba)
            dw1 = jnp.einsum('bco,bch->boh', vi, hidden * l1)
            dw0 = jnp.einsum('bch,bcd->bhd', dgba, ki * l0)
            dw2 = jnp.einsum('bch,bcd->bhd', dhbm, ki * l2)
            mm = jnp.mean(mi, axis=1, keepdims=True)
            dw0 = dw0 + M0 * mm
            dw1 = dw1 + M1 * mm
            dw2 = dw2 + M2 * mm
            M0n, M1n, M2n = (dw0, dw1, dw2)
            dw0 = _newtonschulz5(dw0)
            dw1 = _newtonschulz5(dw1)
            dw2 = _newtonschulz5(dw2)

            def renorm(Wn, n):
                return Wn / (jnp.linalg.norm(Wn, axis=2, keepdims=True) + 1e-05) * n
            return ((renorm(W0 + dw0, n0), renorm(W1 + dw1, n1), renorm(W2 + dw2, n2), M0n, M1n, M2n), out)
        init = (w0b, w1b, w2b, jnp.zeros_like(w0b), jnp.zeros_like(w1b), jnp.zeros_like(w2b))
        _, outs = jax.lax.scan(step, init, xs)
        ttt_out = outs.transpose(1, 0, 2, 3).reshape(b * NH, L, HEAD_DIM)
        ms = jnp.mean(ttt_out * ttt_out, axis=-1, keepdims=True)
        ttt_out = ttt_out * jax.lax.rsqrt(ms + 1e-05) * o_norm_g
        scale = jax.nn.silu(x @ Ws + bs).reshape(b, L, NH, 1)
        scale = scale.transpose(0, 2, 1, 3).reshape(b * NH, L, 1)
        ttt_out = (ttt_out * scale).reshape(b, NH, L, HEAD_DIM)
        ttt_out = ttt_out.transpose(0, 2, 1, 3).reshape(b, L, d)
        aq, ak, av = jnp.split(attn_qkv, 3, axis=-1)
        aq = aq * qk_scale[:, 0] + qk_offset[:, 0]
        ak = ak * qk_scale[:, 1] + qk_offset[:, 1]
        aq = aq.reshape(b, L, NAH, ATTN_HEAD_DIM)
        ak = ak.reshape(b, L, NAH, ATTN_HEAD_DIM)
        av = av.reshape(b, L, NAH, ATTN_HEAD_DIM)
        W_ = WINDOW
        nb = L // W_
        kpad = jnp.pad(ak, ((0, 0), (W_, 0), (0, 0), (0, 0)))
        vpad = jnp.pad(av, ((0, 0), (W_, 0), (0, 0), (0, 0)))
        widx = jnp.arange(nb)[:, None] * W_ + jnp.arange(2 * W_)[None, :]
        kwin = kpad[:, widx]
        vwin = vpad[:, widx]
        qblk = aq.reshape(b, nb, W_, NAH, ATTN_HEAD_DIM)
        scores = jnp.einsum('bnqhd,bnkhd->bnhqk', qblk, kwin) / np.sqrt(ATTN_HEAD_DIM)
        qi_ = jnp.arange(W_)[:, None]
        kj = jnp.arange(2 * W_)[None, :]
        base = (kj >= qi_) & (kj <= qi_ + W_)
        kvalid = jnp.arange(nb)[:, None] * W_ - W_ + jnp.arange(2 * W_)[None, :] >= 0
        mask = base[None, :, :] & kvalid[:, None, :]
        scores = jnp.where(mask[None, :, None], scores, -jnp.inf)
        probs = jax.nn.softmax(scores, axis=-1)
        attn_out = jnp.einsum('bnhqk,bnkhd->bnqhd', probs, vwin).reshape(b, L, d)
        return (ttt_out + attn_out) @ Wo

    def _L0_ffn_ref(hidden_states, gate_w, gate_bias, fc1_w, fc2_w, w1, w2, shared_up_w, shared_down_w):
        import jax, jax.numpy as jnp
        import numpy as np
        H, LAT, INTER, E, G, TOPK_G, TOP_K = (256, 128, 128, 32, 4, 2, 8)
        SHARED_INTER = 512
        ROUTED_SCALE = 2.5
        B, S = (2, 128)

        def relu2(x):
            return jnp.square(jax.nn.relu(x))
        orig_shape = hidden_states.shape
        x = hidden_states.reshape(-1, H)
        T = x.shape[0]
        logits = jnp.einsum('th,eh->te', x.astype(jnp.float32), gate_w)
        scores = jax.nn.sigmoid(logits)
        sb = scores + gate_bias
        grp = sb.reshape(T, G, E // G)
        group_scores = jax.lax.top_k(grp, 2)[0].sum(-1)
        _, gidx = jax.lax.top_k(group_scores, TOPK_G)
        gmask = jax.nn.one_hot(gidx, G, dtype=sb.dtype).sum(1)
        masked = jnp.where(gmask[:, :, None] > 0, grp, -jnp.inf).reshape(T, E)
        _, topi = jax.lax.top_k(masked, TOP_K)
        wsel = jnp.take_along_axis(scores, topi, axis=1)
        wsel = wsel / wsel.sum(-1, keepdims=True) * ROUTED_SCALE
        cw = jnp.zeros((T, E), jnp.float32).at[jnp.arange(T)[:, None], topi].add(wsel)
        x_lat = x @ fc1_w.T
        h = relu2(jnp.einsum('tl,eil->eti', x_lat, w1))
        h = h * cw.T[:, :, None]
        y_lat = jnp.einsum('eti,eli->tl', h, w2)
        routed = y_lat @ fc2_w.T
        shared = relu2(x @ shared_up_w.T) @ shared_down_w.T
        return (shared + routed).reshape(orig_shape)
    x = L0_attn_x
    xn = _layernorm(x, axis=-1)
    x = x + _L0_attn_ref(xn, L0_attn_Wqkv, L0_attn_Wlr, L0_attn_Wm, L0_attn_bm, L0_attn_Ws, L0_attn_bs, L0_attn_Wo, L0_attn_w0, L0_attn_w1, L0_attn_w2, L0_attn_o_norm_g, L0_attn_qk_scale, L0_attn_qk_offset) + _L0_ffn_ref(xn, L0_ffn_gate_w, L0_ffn_gate_bias, L0_ffn_fc1_w, L0_ffn_fc2_w, L0_ffn_w1, L0_ffn_w2, L0_ffn_shared_up_w, L0_ffn_shared_down_w)
    return x

_drawn_inputs = setup_inputs


def setup_inputs(seed=0):
    import zlib

    import numpy as np

    out = dict(_drawn_inputs(seed))
    spreads = {'L0_attn_bm': (0.0, 0.8),
     'L0_attn_bs': (0.0, 2.0),
     'L0_attn_o_norm_g': (1.0, 0.6),
     'L0_attn_qk_scale': (1.0, 0.6),
     'L0_attn_qk_offset': (0.0, 2.0)}
    factors = {'L0_ffn_gate_w': 8.0,
     'L0_ffn_gate_bias': 8.0,
     'L0_ffn_fc1_w': 8.0,
     'L0_ffn_fc2_w': 8.0,
     'L0_ffn_w1': 8.0,
     'L0_ffn_w2': 8.0,
     'L0_attn_Wqkv': 8.0,
     'L0_attn_Wlr': 8.0,
     'L0_attn_Wm': 8.0,
     'L0_attn_Ws': 7.935,
     'L0_attn_Wo': 6.789,
     'L0_attn_w0': 8.0,
     'L0_attn_w1': 8.0,
     'L0_attn_w2': 8.0,
     'L0_ffn_shared_up_w': 8.0,
     'L0_ffn_shared_down_w': 8.0}
    for name, (base, spread) in spreads.items():
        noise = np.random.default_rng([zlib.crc32(name.encode()), seed]).standard_normal(out[name].shape)
        drawn = base * np.exp(spread * noise) if base else spread * noise
        out[name] = jnp.asarray(drawn.astype(out[name].dtype))
    for name, factor in factors.items():
        out[name] = (out[name] * factor).astype(out[name].dtype)
    return out
```

```python
from contextlib import ExitStack

import concourse.bass as bass
from concourse import mybir

ALU = mybir.AluOpType
ACT = mybir.ActivationFunctionType
F32 = mybir.dt.float32
AX_X = mybir.AxisListType.X

P = 128
D = 256
KT = D // P
HD = 64
NH = 4
G = 2
AHD = 128
NAH = D // AHD
E = 32
NG = 4
EPG = E // NG
SH = 512
SC = SH // P
EU = 4
NU = E // EU
W0, W2, W1 = range(3)
LR_INV = -4.600165812166012
ATT_SCALE = AHD ** -0.5
ROUTED_SCALE = 2.5
NEG = -1e30
TAKEN = -2e30
NS = [(4.0848, -6.8946, 2.927), (3.9505, -6.3029, 2.6377), (3.7418, -5.5913, 2.3037),
      (2.8769, -3.1427, 1.2046), (2.8366, -3.0525, 1.2012)]
NI = len(NS)
LR, MOM, SCL, GATE, SMALL = 0, 12, 16, 20, 52


class Expect:

    def __init__(self, eng, sem, name, first=1, step=1):
        self.eng, self.sem, self.step = eng, sem, step
        self.reg = eng.alloc_register(name)
        eng.reg_mov(self.reg, first)

    def wait(self, skip=0):
        self.eng.wait_ge(self.sem, self.reg)
        self.eng.reg_add(self.reg, self.reg, self.step + skip)


def build(nc, x, wqkv, wlr, wm, bm, ws, bs, wo, w0, w1, w2, og, qks, qko, gateT, gbias, fc1T, fc2T,
          e1T, e2T, upT, downT, ident_d, bdones_d, masks_d, out):
    T = x.shape[0]
    NT = T // P
    LAST = NT - 1
    with ExitStack() as ctx:
        def sb(name, shape):
            return ctx.enter_context(nc.sbuf_tensor(name, shape, F32))

        def bank(name):
            return ctx.enter_context(nc.psum_tensor(name, [P, 512], F32))

        def sem(name):
            return ctx.enter_context(nc.semaphore(name))

        wall = sb("wall", [P, KT, 3 * D + SMALL])
        wo_s = sb("wo_s", [P, KT, D])
        fc1_s = sb("fc1_s", [P, KT, P])
        fc2_s = sb("fc2_s", [P, D])
        up_s = sb("up_s", [P, KT, SH])
        down_s = sb("down_s", [P, SC, D])
        e1_s = sb("e1_s", [P, E, P])
        e2_s = sb("e2_s", [P, E, P])
        ident = sb("ident", [P, P])
        bdones = sb("bdones", [P, P])
        ones = sb("ones", [P, P])
        bias = sb("bias", [P, SMALL])
        gb = sb("gb", [P, E])
        og_s = sb("og_s", [P, HD])
        qks_s = sb("qks_s", [P, NAH, 2])
        qko_s = sb("qko_s", [P, NAH, 2])
        mask = sb("mask", [P, 2, P])
        mask_prev = sb("mask_prev", [P, P])
        half = sb("half", [P, 8])
        neghalf = sb("neghalf", [P, 8])
        a_tile = sb("a_tile", [P, NI, 3 * HD])
        Wn = [sb(f"Wn{g}", [P, 3, HD]) for g in range(G)]
        WBD = [sb(f"WBD{g}", [P, 3, P]) for g in range(G)]
        WT = [sb(f"WT{g}", [P, 3, P]) for g in range(G)]
        Mom = [sb(f"Mom{g}", [P, 3, HD]) for g in range(G)]
        nrm = [sb(f"nrm{g}", [P, 3]) for g in range(G)]
        X = [sb(f"X{g}", [P, 3, HD]) for g in range(G)]
        aX = [sb(f"aX{g}", [P, 3, HD]) for g in range(G)]
        XT = [sb(f"XT{g}", [HD, 3, P]) for g in range(G)]
        Am = [sb(f"Am{g}", [P, 3, HD]) for g in range(G)]
        Mp = [sb(f"Mp{g}", [P, 3, HD]) for g in range(G)]
        sq3 = [sb(f"sq3{g}", [P, 3, HD]) for g in range(G)]
        r3 = [sb(f"r3{g}", [P, 6, 3]) for g in range(G)]
        ks = [sb(f"ks{g}", [P, 3, P]) for g in range(G)]
        kt = [sb(f"kt{g}", [P, 4, P]) for g in range(G)]
        dga = [sb(f"dga{g}", [P, P]) for g in range(G)]
        dhb = [sb(f"dhb{g}", [P, P]) for g in range(G)]
        hid = [sb(f"hid{g}", [P, P]) for g in range(G)]
        xa = sb("xa", [P, D])
        xr = sb("xr", [P, D])
        ot = sb("ot", [P, D])
        st6 = sb("st6", [P, 6])
        mv = sb("mv", [P, 2])
        rstd = sb("rstd", [P, 2])
        xn = sb("xn", [P, D])
        xnT = sb("xnT", [P, KT, P])
        raw = sb("raw", [P, 3 * D])
        sig = sb("sig", [P, 3 * D])
        sl = sb("sl", [P, 3 * D])
        sq8 = sb("sq8", [P, 2 * D])
        r8 = sb("r8", [P, 4, 8])
        qkn = sb("qkn", [P, 2 * D])
        z = sb("z", [P, SMALL])
        sgs = sb("sgs", [P, SMALL - MOM])
        lt = sb("lt", [P, 8, 12])
        lr = sb("lr", [P, NH, 3])
        kl0 = sb("kl0", [P, NH, HD])
        kl2 = sb("kl2", [P, NH, HD])
        vl1 = sb("vl1", [P, NH, HD])
        mmc = sb("mmc", [P, G])
        qkT = sb("qkT", [P, 4, P])
        vT = sb("vT", [P, G, P])
        gsig = sb("gsig", [P, G, P])
        gt1 = sb("gt1", [P, G, P])
        gh = sb("gh", [P, G, P])
        to = sb("to", [P, D])
        tsq = sb("tsq", [P, D])
        r4 = sb("r4", [P, 4, 4])
        tt1 = sb("tt1", [P, D])
        ttt = sb("ttt", [P, D])
        aqT = sb("aqT", [P, NAH, P])
        akT = sb("akT", [P, NAH, 2, P])
        vw = sb("vw", [P, 2, D])
        sm = sb("sm", [P, NAH, 2, P])
        pr = sb("pr", [P, NAH, 2, P])
        prT = sb("prT", [P, NAH, 2, P])
        r2 = sb("r2", [P, 4, 2])
        att = sb("att", [P, D])
        comb = sb("comb", [P, D])
        combT = sb("combT", [P, KT, P])
        sbias = sb("sbias", [P, E])
        g8 = sb("g8", [P, NG, 8])
        gs = sb("gs", [P, 12])
        t8 = sb("t8", [P, 8])
        gm = sb("gm", [P, 12])
        pen = sb("pen", [P, NG])
        msk = sb("msk", [P, E])
        m8 = sb("m8", [P, 8])
        mr = sb("mr", [P, E])
        csel = sb("csel", [P, E])
        cs1 = sb("cs1", [P, 2])
        cw = sb("cw", [P, E])
        xlT = sb("xlT", [P, P])
        ur = sb("ur", [P, SC, P])
        us = sb("us", [P, SC, P])
        hr = [sb(f"hr{b}", [P, EU, P]) for b in range(2)]
        hq = [sb(f"hq{b}", [P, EU, P]) for b in range(2)]
        acc = sb("acc", [P, EU, P])
        ya = sb("ya", [P, 2, P])
        ys = sb("ys", [P, P])
        yT = sb("yT", [P, P])

        CA = [bank(f"CA{g}") for g in range(G)]
        CB = [bank(f"CB{g}") for g in range(G)]
        M0 = bank("M0")
        M1 = bank("M1")
        HB = bank("HB")
        YB = bank("YB")

        def per_group(name):
            return [sem(f"{name}{g}") for g in range(G)]

        e_const, e_ffw, e_ttw, e_init = sem("const_in"), sem("ffn_weights_in"), sem("fast_weights_in"), sem("init")
        e_xa, e_xr, e_stored = sem("xa_in"), sem("xr_in"), sem("stored")
        e_stats, e_aggr, e_veps, e_rstd, e_xn = (sem(n) for n in ("stats", "aggr", "veps", "rstd", "xn_ready"))
        e_pt, e_xnT, e_pqa, e_pqb = (sem(n) for n in ("xn_turned", "xnT_ready", "qk_projected", "v_projected"))
        e_rawqk, e_rawv, e_z, e_sgs = (sem(n) for n in ("raw_qk", "raw_v", "z_ready", "sigmoids"))
        e_slqk, e_slv, e_sq8, e_ss8, e_n8, e_r8 = (sem(n) for n in ("silu_qk", "silu_v", "sq8", "ss8", "n8", "r8"))
        e_qkn, e_mm, e_mmc = (sem(n) for n in ("qkn_ready", "mom_summed", "mom_mean"))
        e_pnv, e_pnqk, e_vT, e_qkT = (sem(n) for n in ("v_turned", "qkn_turned", "vT_ready", "qkT_ready"))
        e_lt, e_ex, e_ln, e_lr, e_kl = (sem(n) for n in ("lr_steps", "lr_exp", "lr_ln", "lr_ready", "kl_ready"))
        e_k, e_kc, e_kd, e_ku, e_dgr = (per_group(n) for n in ("k_side", "k_copied", "k_steps", "k_u", "dgba"))
        e_dw, e_G, e_s3, e_ssb, e_sst, e_pw, e_x = (per_group(n) for n in ("dw", "G", "s3", "ssb", "sst", "pw", "X"))
        e_ax, e_t, e_xt, e_am = (per_group(n) for n in ("aX", "turn", "XT", "Am"))
        e_prod, e_mp = (per_group(n) for n in ("product", "Mp"))
        e_up, e_rn, e_rp, e_wn, e_bd, e_wt, e_WT = (per_group(n) for n in ("upd", "rn", "rp", "Wn", "WBD", "wt", "WT"))
        e_qs, e_gsig, e_gt1, e_gh, e_qo, e_to = (sem(n) for n in ("q_side", "gate_sig", "gt1", "gh", "q_out", "to_copied"))
        e_msq, e_rms, e_tf, e_ttt = (sem(n) for n in ("ms", "rms", "ttt_steps", "ttt_ready"))
        e_at, e_aT, e_win, e_as, e_sm, e_nb, e_pr = (sem(n) for n in ("raw_turned", "aT", "window", "scores", "masked", "negmax", "probs"))
        e_ap, e_prT, e_av, e_at2, e_comb, e_ct, e_combT = (sem(n) for n in ("probs_turned", "prT", "att_pv", "att_steps", "comb", "comb_turned", "combT"))
        e_mask = sem("mask_ready")
        e_rt, e_cw = sem("route_steps"), sem("cw_ready")
        e_lr_steps, e_nmx, e_rf = sem("lr_sum_steps"), sem("max_ready"), per_group("rf")
        e_fx, e_xlT, e_upm, e_ur, e_us = (sem(n) for n in ("fc1", "xlT", "shared_up", "shared_relu", "shared_sq"))
        e_h, e_hr, e_hq, e_y, e_acc = (sem(n) for n in ("h", "h_relu", "h_sq", "y", "acc"))
        e_ya, e_ys, e_yt, e_yT, e_out, e_ot = (sem(n) for n in ("ya", "y_sum", "y_turned", "yT", "out_mm", "out_ready"))

        NCONST, NFFW, NTTW = 16, 6, 3

        block = ctx.enter_context(nc.Block())

        @block.sync
        def _(sp):
            sp.dma_start(xa[:, :], x[0:P, :]).then_inc(e_xa, 16)
            consts = [(ident[:, :], ident_d[:, :]), (wall[:, :, 0:3 * D], wqkv.rearrange("(k p) n -> p k n", p=P)),
                      (bdones[:, :], bdones_d[:, :]),
                      (mask[:, :, :], masks_d[:, 0:2, :]), (mask_prev[:, :], masks_d[:, 2, :])]
            small = [(wlr, LR, MOM), (wm, MOM, SCL), (ws, SCL, GATE), (gateT, GATE, SMALL)]
            consts += [(wall[:, :, 3 * D + a:3 * D + b], w.rearrange("(k p) n -> p k n", p=P)) for w, a, b in small]
            consts += [(bias[:, MOM:SCL], bm.partition_broadcast(P)), (bias[:, SCL:GATE], bs.partition_broadcast(P)),
                       (gb[:, :], gbias.partition_broadcast(P)), (og_s[:, :], og.partition_broadcast(P)),
                       (qks_s[:, :, :], qks.rearrange("(h p) c -> p h c", p=P)),
                       (qko_s[:, :, :], qko.rearrange("(h p) c -> p h c", p=P)),
                       (wo_s[:, :, :], wo.rearrange("(k p) n -> p k n", p=P))]
            assert len(consts) == NCONST
            for dst, src in consts:
                sp.dma_start(dst, src).then_inc(e_const, 16)
            sp.wait_ge(e_xn, 1)
            sp.dma_start(xa[:, :], x[P:2 * P, :]).then_inc(e_xa, 16)
            sp.dma_start(xr[:, :], x[0:P, :]).then_inc(e_xr, 16)

            def store(i, rows):
                sp.wait_ge(e_ot, i + 1)
                sp.dma_start(out[bass.ds(rows, P), :], ot[:, :]).then_inc(e_stored, 16)

            with sp.Fori(0, NT - 2) as i:
                here, after, later = sp.snap(i * P), sp.snap((i + 1) * P), sp.snap((i + 2) * P)
                sp.wait_ge(e_xn, i + 2)
                sp.dma_start(xa[:, :], x[bass.ds(later, P), :]).then_inc(e_xa, 16)
                store(i, here)
                sp.dma_start(xr[:, :], x[bass.ds(after, P), :]).then_inc(e_xr, 16)
            store(NT - 2, (NT - 2) * P)
            sp.dma_start(xr[:, :], x[LAST * P:T, :]).then_inc(e_xr, 16)
            store(LAST, LAST * P)
            sp.wait_ge(e_stored, 16 * NT)

        @block.gpsimd
        def _(pool):
            for w, (n, src) in enumerate((("W0", w0), ("W2", w2), ("W1", w1))):
                for g in range(G):
                    pool.dma_start(Wn[g][:, w, :], src[2 * g:2 * g + 2].rearrange("h r c -> (h r) c")).then_inc(e_ttw, 16)
            for dst, src in ((fc1_s[:, :, :], fc1T.rearrange("(k p) n -> p k n", p=P)),
                             (up_s[:, :, :], upT.rearrange("(k p) n -> p k n", p=P)),
                             (e1_s[:, :, :], e1T), (e2_s[:, :, :], e2T),
                             (down_s[:, :, :], downT.rearrange("(k p) n -> p k n", p=P)), (fc2_s[:, :], fc2T)):
                pool.dma_start(dst, src).then_inc(e_ffw, 16)
            win_scores = Expect(pool, e_as, "win_scores", first=2)
            win_pv = Expect(pool, e_av, "win_pv", first=2)
            win_raw = Expect(pool, e_rawv, "win_raw", first=3)
            win_vw = Expect(pool, e_win, "win_vw", first=5, step=2)
            pool.wait_ge(e_init, 1)

            def power(dst, src, expo, n):
                return pool.tensor_tensor(dst, src, expo[:, 0:n], ALU.pow)

            def prep_rstd(m):
                pool.wait_ge(e_veps, m + 1)
                power(rstd[:, 0:1], rstd[:, 1:2], neghalf, 1).then_inc(e_rstd, 1)

            def prep_n8(m):
                pool.wait_ge(e_ss8, m + 1)
                power(r8[:, 1, :], r8[:, 0, :], half, 8).then_inc(e_n8, 1)

            def prep_kl(m):
                pool.wait_ge(e_lr, m + 1)
                for g in range(G):
                    pool.wait_ge(e_dw[g], m)
                kk = qkn[:, D:2 * D].rearrange("p (h c) -> p h c", c=HD)
                vv = sl[:, 2 * D:3 * D].rearrange("p (h c) -> p h c", c=HD)
                for dst, src, n in ((kl0, kk, 0), (kl2, kk, 2), (vl1, vv, 1)):
                    ins = pool.tensor_tensor(dst[:, :, :], src, lr[:, :, n:n + 1].to_broadcast([P, NH, HD]), ALU.mult)
                ins.then_inc(e_kl, 1)

            def window(m, known):
                if known:
                    pool.wait_ge(e_as, m)
                    pool.wait_ge(e_av, m)
                    pool.wait_ge(e_rawv, m + 1)
                else:
                    win_scores.wait()
                    win_pv.wait()
                    win_raw.wait()
                pool.tensor_copy(akT[:, :, 0, :], akT[:, :, 1, :])
                pool.tensor_copy(vw[:, 0, :], vw[:, 1, :]).then_inc(e_win, 1)
                if known:
                    pool.wait_ge(e_win, 2 * m + 1)
                else:
                    win_vw.wait()
                pool.tensor_copy(vw[:, 1, :], raw[:, 2 * D:3 * D]).then_inc(e_win, 1)

            def restore_mask():
                pool.wait_ge(e_sm, 1)
                pool.tensor_copy(mask[:, 0, :], mask_prev[:, :]).then_inc(e_mask, 1)

            def k_u(i, g):
                pool.wait_ge(e_kc[g], i + 1)
                pool.tensor_tensor(kt[g][:, 3, :], ks[g][:, 1, :], ks[g][:, 2, :], ALU.mult).then_inc(e_ku[g], 1)

            def ss_pow(i, g):
                pool.wait_ge(e_sst[g], 3 * i + 1)
                power(r3[g][:, 2, :], r3[g][:, 1, :], half, 3).then_inc(e_pw[g], 1)

            def ax(i, g, it):
                pool.wait_ge(e_x[g], (NI + 1) * i + it + 1)
                pool.tensor_tensor(aX[g][:, :, :].rearrange("p w c -> p (w c)"),
                                   X[g][:, :, :].rearrange("p w c -> p (w c)"), a_tile[:, it, :],
                                   ALU.mult).then_inc(e_ax[g], 1)

            def row_pow(m, g):
                pool.wait_ge(e_rn[g], m + 1)
                power(r3[g][:, 4, :], r3[g][:, 3, :], half, 3).then_inc(e_rp[g], 1)

            def rms_pow(i):
                pool.wait_ge(e_msq, 2 * i + 2)
                power(r4[:, 1, :], r4[:, 0, :], neghalf, 4).then_inc(e_rms, 1)

            def shared_sq(i):
                pool.wait_ge(e_ur, i + 1)
                pool.tensor_tensor(us[:, :, :], ur[:, :, :], ur[:, :, :], ALU.mult).then_inc(e_us, 1)

            def h_sq(i, u):
                pool.wait_ge(e_hr, NU * i + u + 1)
                if u > 1 or not (isinstance(i, int) and i == 0):
                    pool.wait_ge(e_y, NU * i + u - 1)
                b = u % 2
                pool.tensor_tensor(hq[b][:, :, :], hr[b][:, :, :], hr[b][:, :, :], ALU.mult).then_inc(e_hq, 1)

            def body(i, last):
                if last:
                    h_sq(i, 0)
                    shared_sq(i)
                    h_sq(i, 1)
                    rms_pow(i)
                    for u in range(2, NU):
                        h_sq(i, u)
                    return
                m = i + 1
                first = isinstance(i, int)
                k_u(i, 0)
                k_u(i, 1)
                h_sq(i, 0)
                h_sq(i, 1)
                for g in range(G):
                    ss_pow(i, g)
                prep_rstd(m)
                h_sq(i, 2)
                fill = {0: [lambda: shared_sq(i)], 2: [lambda: h_sq(i, 3)], 3: [lambda: rms_pow(i)],
                        7: [lambda: h_sq(i, 4)], 9: [lambda: prep_n8(m), lambda: h_sq(i, 5)],
                        12: [lambda: h_sq(i, 6)], 14: [lambda: h_sq(i, 7)], 15: [lambda: window(m, first)],
                        17: [lambda: prep_kl(m)]}
                if first:
                    fill[13] = [restore_mask]
                for st in range(4 * NI):
                    if st % 4 == 0:
                        for g in range(G):
                            ax(i, g, st // 4)
                    for f in fill.get(st, []):
                        f()
                for g in range(G):
                    row_pow(m, g)

            for g in range(G):
                row_pow(0, g)
            prep_rstd(0)
            prep_n8(0)
            prep_kl(0)
            window(0, True)
            body(0, False)
            with pool.Fori(1, LAST) as i:
                body(i, False)
            body(LAST, True)

        @block.scalar
        def _(act):
            act.wait_ge(e_const, 16 * NCONST)

            def a(out_, in_, func, **kw):
                return nc.scalar.activation(out_, in_, func, **kw)

            def prep_xnT(m):
                act.wait_ge(e_pt, m + 1)
                a(xnT[:, :, :].rearrange("p k t -> p (k t)"), M0[:, 0:D], ACT.Copy).then_inc(e_xnT, 1)

            def prep_qk(m):
                act.wait_ge(e_pqa, m + 1)
                act.wait_ge(e_at, m)
                act.wait_ge(e_slv, m)
                a(sig[:, 0:2 * D], M0[:, :], ACT.Sigmoid)
                a(raw[:, 0:2 * D], M0[:, :], ACT.Copy).then_inc(e_rawqk, 1)

            def prep_v(m):
                act.wait_ge(e_pqb, m + 1)
                act.wait_ge(e_win, 2 * m)
                a(sig[:, 2 * D:3 * D], M1[:, 0:D], ACT.Sigmoid)
                a(raw[:, 2 * D:3 * D], M1[:, 0:D], ACT.Copy).then_inc(e_rawv, 1)

            def prep_small(m):
                act.wait_ge(e_z, m + 1)
                act.wait_ge(e_cw, m)
                act.wait_ge(e_ttt, m)
                a(sgs[:, :], z[:, MOM:SMALL], ACT.Sigmoid).then_inc(e_sgs, 1)

            def prep_sq8(m):
                act.wait_ge(e_slqk, m + 1)
                a(sq8[:, :], sl[:, 0:2 * D], ACT.Square).then_inc(e_sq8, 1)

            def prep_vT(m):
                act.wait_ge(e_pnv, m + 1)
                a(vT[:, :, :].rearrange("p g t -> p (g t)"), M0[:, 0:D], ACT.Copy).then_inc(e_vT, 1)

            def prep_qkT(m):
                act.wait_ge(e_pnqk, m + 1)
                a(qkT[:, :, :].rearrange("p g t -> p (g t)"), M1[:, :], ACT.Copy).then_inc(e_qkT, 1)

            def lr_exp(m):
                act.wait_ge(e_lt, 3 * m + 1)
                a(lt[:, 1, :], lt[:, 0, :], ACT.Exp).then_inc(e_ex, 1)

            def lr_ln(m):
                act.wait_ge(e_lt, 3 * m + 2)
                a(lt[:, 3, :], lt[:, 2, :], ACT.Ln).then_inc(e_ln, 1)

            def k_side(i, g):
                act.wait_ge(e_k[g], i + 1)
                a(ks[g][:, 0, :], CB[g][:, 0:P], ACT.Sigmoid)
                a(ks[g][:, 1:3, :].rearrange("p w c -> p (w c)"), CB[g][:, P:3 * P], ACT.Copy).then_inc(e_kc[g], 1)

            def xt(i, g, it):
                act.wait_ge(e_t[g], NI * i + it + 1)
                a(XT[g][:, :, :].rearrange("p w c -> p (w c)"), CA[g][0:HD, 0:3 * P], ACT.Copy).then_inc(e_xt[g], 1)

            def w_bd(m, g):
                act.wait_ge(e_wn[g], m)
                a(WBD[g][0:HD, :, 0:HD], Wn[g][0:HD, :, :], ACT.Copy)
                a(WBD[g][HD:P, :, HD:P], Wn[g][HD:P, :, :], ACT.Copy).then_inc(e_bd[g], 1)

            def w_T(m, g):
                act.wait_ge(e_wt[g], m + 1)
                a(WT[g][:, :, :].rearrange("p w c -> p (w c)"), CA[g][:, 0:3 * P], ACT.Copy).then_inc(e_WT[g], 1)

            def gate_sig(i):
                act.wait_ge(e_qs, i + 1)
                a(gsig[:, :, :], M0[:, :].rearrange("p (g w t) -> p g w t", g=G, w=2)[:, :, 0, :], ACT.Sigmoid)\
                    .then_inc(e_gsig, 1)

            def q_out(i):
                act.wait_ge(e_qo, i + 1)
                a(to[:, :], M1[:, 0:D], ACT.Copy)
                a(tsq[:, :], M1[:, 0:D], ACT.Square).then_inc(e_to, 1)

            def x_lat(m):
                act.wait_ge(e_fx, m + 1)
                act.wait_ge(e_h, NU * m)
                a(xlT[:, :], M1[:, 0:P], ACT.Copy).then_inc(e_xlT, 1)

            def shared_relu(i):
                act.wait_ge(e_upm, i + 1)
                a(ur[:, :, :].rearrange("p s t -> p (s t)"), M0[:, :], ACT.Relu).then_inc(e_ur, 1)

            def h_relu(i, u):
                act.wait_ge(e_h, NU * i + u + 1)
                if u > 1 or not (isinstance(i, int) and i == 0):
                    act.wait_ge(e_hq, NU * i + u - 1)
                a(hr[u % 2][:, :, :].rearrange("p s t -> p (s t)"), HB[:, :], ACT.Relu).then_inc(e_hr, 1)

            def probs(i):
                act.wait_ge(e_nb, i + 1)
                for h in range(NAH):
                    ins = a(pr[:, h].rearrange("p w k -> p (w k)"), sm[:, h].rearrange("p w k -> p (w k)"), ACT.Exp,
                            bias=r2[:, 1, h:h + 1], scale=ATT_SCALE, accum_out=r2[:, 2, h:h + 1])
                ins.then_inc(e_pr, 1)

            def probs_T(i):
                act.wait_ge(e_ap, i + 1)
                a(prT[:, :, :, :].rearrange("p h w k -> p (h w k)"), M1[:, :], ACT.Copy).then_inc(e_prT, 1)

            def comb_T(i):
                act.wait_ge(e_ct, i + 1)
                a(combT[:, :, :].rearrange("p h k -> p (h k)"), M1[:, 0:D], ACT.Copy).then_inc(e_combT, 1)

            def y_T(i):
                act.wait_ge(e_yt, i + 1)
                a(yT[:, :], M1[:, 0:P], ACT.Copy).then_inc(e_yT, 1)

            def body(i, last):
                if last:
                    gate_sig(i)
                    h_relu(i, 1)
                    shared_relu(i)
                    q_out(i)
                    act.preload_act_table_set("natural_log_exp_and_others")
                    probs(i)
                    h_relu(i, 2)
                    probs_T(i)
                    for u in range(3, NU - 1):
                        h_relu(i, u)
                    comb_T(i)
                    h_relu(i, NU - 1)
                    y_T(i)
                    return
                m = i + 1
                k_side(i, 0)
                k_side(i, 1)
                h_relu(i, 1)
                gate_sig(i)
                h_relu(i, 2)

                def to_exp():
                    act.preload_act_table_set("natural_log_exp_and_others")

                def to_sigmoid():
                    act.preload_act_table_set("sigmoid_and_others")

                shared_relu(i)
                fill = {0: [lambda: h_relu(i, 3)], 2: [lambda: q_out(i), lambda: prep_xnT(m)],
                        5: [lambda: prep_qk(m)], 6: [lambda: prep_v(m)], 7: [lambda: h_relu(i, 4), lambda: prep_small(m)],
                        8: [lambda: prep_sq8(m)], 9: [lambda: prep_vT(m), lambda: h_relu(i, 5), to_exp],
                        11: [lambda: lr_exp(m)], 12: [lambda: probs(i), lambda: prep_qkT(m), lambda: h_relu(i, 6)],
                        13: [lambda: lr_ln(m)], 14: [lambda: probs_T(i), lambda: h_relu(i, 7)], 15: [to_sigmoid],
                        17: [lambda: comb_T(i)], 19: [lambda: x_lat(m)]}
                for st in range(4 * NI):
                    if st % 4 == 0:
                        for g in range(G):
                            xt(i, g, st // 4)
                    for f in fill.get(st, []):
                        f()
                y_T(i)
                h_relu(m, 0)
                for g in range(G):
                    w_bd(m, g)
                for g in range(G):
                    w_T(m, g)

            act.wait_ge(e_init, 1)
            act.wait_ge(e_ttw, 16 * NTTW * G)
            for g in range(G):
                w_bd(0, g)
            for g in range(G):
                w_T(0, g)
            prep_xnT(0)
            prep_qk(0)
            prep_v(0)
            prep_small(0)
            prep_sq8(0)
            prep_vT(0)
            prep_qkT(0)
            x_lat(0)
            h_relu(0, 0)
            act.preload_act_table_set("natural_log_exp_and_others")
            lr_exp(0)
            lr_ln(0)
            body(0, False)
            with act.Fori(1, LAST) as i:
                body(i, False)
            body(LAST, True)

        @block.tensor
        def _(pe):
            x_turn = [Expect(pe, e_x[g], f"x_turn{g}") for g in range(G)]
            xt_in = [Expect(pe, e_xt[g], f"xt_in{g}") for g in range(G)]
            am_in = [Expect(pe, e_am[g], f"am_in{g}") for g in range(G)]
            mp_in = [Expect(pe, e_mp[g], f"mp_in{g}") for g in range(G)]
            d_in = [Expect(pe, e_dgr[g], f"d_in{g}") for g in range(G)]
            kl_in = Expect(pe, e_kl, "kl_in")
            pe.wait_ge(e_const, 16 * NCONST)
            pe.wait_ge(e_init, 1)

            def mm(out_, lhsT, rhs, start=True, stop=True):
                return pe.matmul(out_, lhsT, rhs, start=start, stop=stop)

            def prep_turn(m):
                pe.wait_ge(e_xn, m + 1)
                pe.wait_ge(e_ur, m)
                for k in range(KT):
                    ins = pe.transpose(M0[:, k * P:(k + 1) * P], xn[:, k * P:(k + 1) * P], ident[:, :])
                ins.then_inc(e_pt, 1)

            def prep_qk(m):
                pe.wait_ge(e_xnT, m + 1)
                mm(M0[:, :], xnT[:, 0, :], wall[:, 0, 0:2 * D], True, False)

            def prep_qk_more(m):
                for k in range(1, KT):
                    ins = mm(M0[:, :], xnT[:, k, :], wall[:, k, 0:2 * D], False, k == KT - 1)
                ins.then_inc(e_pqa, 1)

            def prep_v(m):
                pe.wait_ge(e_to, m)
                for k in range(KT):
                    ins = mm(M1[:, 0:D + SMALL], xnT[:, k, :], wall[:, k, 2 * D:3 * D + SMALL], k == 0, k == KT - 1)
                ins.then_inc(e_pqb, 1)

            def prep_mom(m):
                pe.wait_ge(e_sgs, m + 1)
                mm(M1[:, 0:NH], ones[:, :], sgs[:, 0:NH]).then_inc(e_mm, 1)

            def prep_turn_v(m):
                pe.wait_ge(e_slv, m + 1)
                pe.wait_ge(e_rawqk, m + 1)
                for g in range(G):
                    ins = pe.transpose(M0[:, g * P:(g + 1) * P], sl[:, 2 * D + g * P:2 * D + (g + 1) * P], ident[:, :])
                ins.then_inc(e_pnv, 1)

            def prep_turn_qk(m):
                pe.wait_ge(e_qkn, m + 1)
                pe.wait_ge(e_mmc, m + 1)
                for n in range(4):
                    ins = pe.transpose(M1[:, n * P:(n + 1) * P], qkn[:, n * P:(n + 1) * P], ident[:, :])
                ins.then_inc(e_pnqk, 1)

            def k_side(i, g):
                pe.wait_ge(e_qkT, i + 1)
                pe.wait_ge(e_vT, i + 1)
                pe.wait_ge(e_WT[g], i + 1)
                mm(CB[g][:, 0:2 * P], qkT[:, 2 + g, :], WT[g][:, W0:W2 + 1, :].rearrange("p w c -> p (w c)"))
                mm(CB[g][:, 2 * P:3 * P], vT[:, g, :], WBD[g][:, W1, :]).then_inc(e_k[g], 1)

            def grads(i, g):
                if g == 0:
                    kl_in.wait()
                d_in[g].wait()
                for h in range(2):
                    c = slice(h * HD, (h + 1) * HD)
                    mm(CA[g][c, 0:HD], dga[g][:, c], kl0[:, 2 * g + h, :])
                    mm(CA[g][c, HD:2 * HD], dhb[g][:, c], kl2[:, 2 * g + h, :])
                    ins = mm(CA[g][c, 2 * HD:3 * HD], vl1[:, 2 * g + h, :], hid[g][:, c])
                ins.then_inc(e_dw[g], 1)

            def sums(i, g):
                pe.wait_ge(e_s3[g], 2 * i + 2)
                mm(CB[g][:, 0:3], bdones[:, :], r3[g][:, 0, :]).then_inc(e_ssb[g], 1)

            def ns_turn(g, last_step):
                x_turn[g].wait(skip=1 if last_step else 0)
                for w in range(3):
                    ins = pe.transpose(CA[g][0:HD, w * P:(w + 1) * P], X[g][:, w, :], ident[:, :])
                ins.then_inc(e_t[g], 1)

            def ns_gram(g):
                xt_in[g].wait()
                for w in range(3):
                    for h in range(2):
                        c = slice(h * HD, (h + 1) * HD)
                        ins = mm(CB[g][c, w * HD:(w + 1) * HD], XT[g][:, w, c], XT[g][:, w, c])
                ins.then_inc(e_prod[g], 1)

            def ns_pair(g, bank_, ready, left, right):
                ready[g].wait()
                for w in range(3):
                    for h in range(2):
                        c = slice(h * HD, (h + 1) * HD)
                        ins = mm(bank_[g][c, w * HD:(w + 1) * HD], left[g][c, w, :], right[g][c, w, :])
                ins.then_inc(e_prod[g], 1)

            def turn_w(m, g):
                pe.wait_ge(e_bd[g], m + 1)
                for w in range(3):
                    ins = pe.transpose(CA[g][:, w * P:(w + 1) * P], WBD[g][:, w, :], ident[:, :])
                ins.then_inc(e_wt[g], 1)

            def q_side(i):
                pe.wait_ge(e_ot, i)
                for g in range(G):
                    pe.wait_ge(e_WT[g], i + 1)
                pe.wait_ge(e_qkT, i + 1)
                for g in range(G):
                    for n, w in enumerate((W0, W2)):
                        ins = mm(M0[:, (2 * g + n) * P:(2 * g + n + 1) * P], WT[g][:, w, :], qkT[:, g, :])
                ins.then_inc(e_qs, 1)

            def q_out(i):
                pe.wait_ge(e_gh, i + 1)
                pe.wait_ge(e_aT, i + 1)
                for g in range(G):
                    ins = mm(M1[:, g * P:(g + 1) * P], gh[:, g, :], WT[g][:, W1, :])
                ins.then_inc(e_qo, 1)

            def att_turn(i):
                pe.wait_ge(e_yT, i)
                pe.wait_ge(e_xlT, i + 1)
                pe.wait_ge(e_rawqk, i + 1)
                for n in range(4):
                    ins = pe.transpose(M1[:, n * P:(n + 1) * P], raw[:, n * P:(n + 1) * P], ident[:, :])
                ins.then_inc(e_at, 1)

            def att_scores(i, last):
                pe.wait_ge(e_aT, i + 1)
                pe.wait_ge(e_win, 2 * i + 2)
                if last:
                    pe.wait_ge(e_ur, i + 1)
                else:
                    pe.wait_ge(e_vT, i + 2)
                for h in range(NAH):
                    ins = mm(M0[:, h * 2 * P:(h + 1) * 2 * P], aqT[:, h, :], akT[:, h].rearrange("p w k -> p (w k)"))
                ins.then_inc(e_as, 1)

            def att_turn_p(i, last):
                pe.wait_ge(e_pr, i + 1)
                if last:
                    pe.wait_ge(e_to, i + 1)
                else:
                    pe.wait_ge(e_qkT, i + 2)
                for h in range(NAH):
                    for w in range(2):
                        n = 2 * h + w
                        ins = pe.transpose(M1[:, n * P:(n + 1) * P], pr[:, h, w, :], ident[:, :])
                ins.then_inc(e_ap, 1)

            def att_pv(i):
                pe.wait_ge(e_prT, i + 1)
                for h in range(NAH):
                    for w in range(2):
                        ins = mm(M0[:, h * P:(h + 1) * P], prT[:, h, w, :], vw[:, w, h * P:(h + 1) * P], w == 0, w == 1)
                ins.then_inc(e_av, 1)

            def turn_comb(i):
                pe.wait_ge(e_comb, i + 1)
                pe.wait_ge(e_prT, i + 1)
                for k in range(KT):
                    ins = pe.transpose(M1[:, k * P:(k + 1) * P], comb[:, k * P:(k + 1) * P], ident[:, :])
                ins.then_inc(e_ct, 1)

            def fc1(m):
                pe.wait_ge(e_xnT, m + 1)
                if isinstance(m, int) and m == 0:
                    pe.wait_ge(e_qkT, 1)
                else:
                    pe.wait_ge(e_combT, m)
                for k in range(KT):
                    ins = mm(M1[:, 0:P], fc1_s[:, k, :], xnT[:, k, :], k == 0, k == KT - 1)
                ins.then_inc(e_fx, 1)

            def shared_up(i, part):
                if part == 0:
                    pe.wait_ge(e_gh, i + 1)
                for c in range(part * SC // 2, (part + 1) * SC // 2):
                    for k in range(KT):
                        ins = mm(M0[:, c * P:(c + 1) * P], up_s[:, k, c * P:(c + 1) * P], xnT[:, k, :], k == 0, k == KT - 1)
                if part == 1:
                    ins.then_inc(e_upm, 1)

            def h_up(i, u):
                if u == 0:
                    pe.wait_ge(e_xlT, i + 1)
                pe.wait_ge(e_hr, NU * i + u)
                for e in range(EU):
                    ins = mm(HB[:, e * P:(e + 1) * P], e1_s[:, EU * u + e, :], xlT[:, :])
                ins.then_inc(e_h, 1)

            def y_down(i, u):
                pe.wait_ge(e_hq, NU * i + u + 1)
                pe.wait_ge(e_acc, NU * i + u)
                for e in range(EU):
                    ins = mm(YB[:, e * P:(e + 1) * P], hq[u % 2][:, e, :], e2_s[:, EU * u + e, :])
                ins.then_inc(e_y, 1)

            def turn_y(i, last):
                pe.wait_ge(e_ys, i + 1)
                if last:
                    pe.wait_ge(e_combT, i + 1)
                else:
                    pe.wait_ge(e_xlT, i + 2)
                pe.transpose(M1[:, 0:P], ys[:, :], ident[:, :]).then_inc(e_yt, 1)

            def out_down(i, part):
                if part == 0:
                    pe.wait_ge(e_comb, i + 1)
                    pe.wait_ge(e_us, i + 1)
                for c in range(part * SC // 2, (part + 1) * SC // 2):
                    mm(M0[:, 0:D], us[:, c, :], down_s[:, c, :], c == 0, False)

            def out_wo(i):
                pe.wait_ge(e_combT, i + 1)
                for k in range(KT):
                    mm(M0[:, 0:D], combT[:, k, :], wo_s[:, k, :], False, False)

            def out_fc2(i):
                pe.wait_ge(e_yT, i + 1)
                mm(M0[:, 0:D], yT[:, :], fc2_s[:, :], False, True).then_inc(e_out, 1)

            def body(i, last):
                if last:
                    q_side(i)
                    att_turn(i)
                    h_up(i, 1)
                    y_down(i, 0)
                    shared_up(i, 0)
                    shared_up(i, 1)
                    q_out(i)
                    att_scores(i, True)
                    h_up(i, 2)
                    y_down(i, 1)
                    att_turn_p(i, True)
                    for u in range(3, NU - 1):
                        h_up(i, u)
                        y_down(i, u - 1)
                        if u == 3:
                            att_pv(i)
                    turn_comb(i)
                    h_up(i, NU - 1)
                    y_down(i, NU - 2)
                    out_down(i, 0)
                    out_down(i, 1)
                    y_down(i, NU - 1)
                    out_wo(i)
                    turn_y(i, True)
                    out_fc2(i)
                    return
                m = i + 1
                k_side(i, 0)
                k_side(i, 1)
                h_up(i, 1)
                q_side(i)
                att_turn(i)
                grads(i, 0)
                y_down(i, 0)
                grads(i, 1)
                h_up(i, 2)
                sums(i, 0)
                sums(i, 1)
                shared_up(i, 0)
                shared_up(i, 1)
                fill = {0: [lambda: h_up(i, 3)], 1: [lambda: y_down(i, 1)],
                        2: [lambda: q_out(i), lambda: prep_turn(m)], 3: [lambda: y_down(i, 2)],
                        4: [lambda: prep_qk(m)], 5: [lambda: prep_qk_more(m)], 6: [lambda: prep_v(m)],
                        7: [lambda: h_up(i, 4)], 8: [lambda: y_down(i, 3), lambda: prep_mom(m)],
                        9: [lambda: prep_turn_v(m), lambda: h_up(i, 5)], 10: [lambda: att_scores(i, False)],
                        11: [lambda: y_down(i, 4)], 12: [lambda: prep_turn_qk(m), lambda: h_up(i, 6)],
                        13: [lambda: y_down(i, 5)], 14: [lambda: att_turn_p(i, False), lambda: h_up(i, 7)],
                        15: [lambda: att_pv(i)], 16: [lambda: y_down(i, 6)],
                        17: [lambda: turn_comb(i), lambda: y_down(i, 7)], 18: [lambda: out_down(i, 0)],
                        19: [lambda: fc1(m), lambda: out_down(i, 1)]}
                for st in range(4 * NI):
                    for g in range(G):
                        if st % 4 == 0:
                            ns_turn(g, st // 4 == NI - 1)
                        elif st % 4 == 1:
                            ns_gram(g)
                        elif st % 4 == 2:
                            ns_pair(g, CA, am_in, Am, Am)
                        else:
                            ns_pair(g, CB, mp_in, Mp, X)
                    for f in fill.get(st, []):
                        f()
                out_wo(i)
                turn_y(i, False)
                h_up(m, 0)
                out_fc2(i)
                for g in range(G):
                    turn_w(m, g)

            for g in range(G):
                turn_w(0, g)
            prep_turn(0)
            prep_qk(0)
            prep_qk_more(0)
            prep_v(0)
            prep_mom(0)
            prep_turn_v(0)
            prep_turn_qk(0)
            pe.wait_ge(e_ffw, 16 * NFFW)
            fc1(0)
            h_up(0, 0)
            body(0, False)
            with pe.Fori(1, LAST) as i:
                body(i, False)
            body(LAST, True)

        @block.vector
        def _(dve):
            nc.vector.memset(ones[:, :], 1.0)
            nc.vector.memset(half[:, :], 0.5)
            nc.vector.memset(neghalf[:, :], -0.5)
            for it in range(NI):
                nc.vector.memset(a_tile[:, it, :], NS[it][0])
            nc.vector.memset(bias[:, LR:MOM], LR_INV)
            nc.vector.memset(bias[:, GATE:SMALL], 0.0)
            nc.vector.memset(gs[:, NG:12], NEG)
            nc.vector.memset(akT[:, :, 1, :], 0.0)
            nc.vector.memset(vw[:, 1, :], 0.0)
            for g in range(G):
                nc.vector.memset(Mom[g][:, :, :], 0.0)
                nc.vector.memset(WBD[g][:, :, :], 0.0)
            nc.vector.memset(lt[:, :, :], 0.0).then_inc(e_init, 1)
            aggr_in = Expect(dve, e_stats, "aggr_in")
            rt = Expect(dve, e_rt, "route_step")
            dve.wait_ge(e_init, 1)
            dve.wait_ge(e_const, 16 * NCONST)

            def heads(t, n):
                return t.rearrange("p (h c) -> p h c", h=n)

            def ln_stats(m):
                dve.wait_ge(e_xa, 16 * m + 16)
                nc.vector.bn_stats(st6[:, :], xa[:, :]).then_inc(e_stats, 1)
                aggr_in.wait()
                nc.vector.bn_aggr(mv[:, :], st6[:, :]).then_inc(e_aggr, 1)
                dve.wait_ge(e_aggr, m + 1)
                nc.vector.tensor_scalar(rstd[:, 1:2], mv[:, 1:2], 1e-5, None, ALU.add).then_inc(e_veps, 1)

            def ln_norm(m):
                dve.wait_ge(e_rstd, m + 1)
                dve.wait_ge(e_pt, m)
                nc.vector.tensor_scalar(xn[:, :], xa[:, :], mv[:, 0:1], rstd[:, 0:1], ALU.subtract, ALU.mult)\
                    .then_inc(e_xn, 1)

            def prep_z(m):
                dve.wait_ge(e_rawv, m + 1)
                nc.vector.tensor_tensor(z[:, :], M1[:, D:D + SMALL], bias[:, :], ALU.add).then_inc(e_z, 1)

            def prep_silu_qk(m):
                dve.wait_ge(e_rawqk, m + 1)
                nc.vector.tensor_tensor(sl[:, 0:2 * D], raw[:, 0:2 * D], sig[:, 0:2 * D], ALU.mult).then_inc(e_slqk, 1)

            def prep_silu_v(m):
                dve.wait_ge(e_kl, m)
                dve.wait_ge(e_pnv, m)
                nc.vector.tensor_tensor(sl[:, 2 * D:3 * D], raw[:, 2 * D:3 * D], sig[:, 2 * D:3 * D], ALU.mult)\
                    .then_inc(e_slv, 1)

            def prep_ss8(m):
                dve.wait_ge(e_sq8, m + 1)
                nc.vector.tensor_reduce(r8[:, 0, :], heads(sq8[:, :], 8), AX_X, ALU.add).then_inc(e_ss8, 1)

            def prep_qkn(m):
                dve.wait_ge(e_n8, m + 1)
                nc.vector.tensor_scalar(r8[:, 2, :], r8[:, 1, :], 1e-5, None, ALU.add).then_inc(e_r8, 1)
                dve.wait_ge(e_r8, 2 * m + 1)
                nc.vector.reciprocal(r8[:, 3, :], r8[:, 2, :]).then_inc(e_r8, 1)
                dve.wait_ge(e_r8, 2 * m + 2)
                dve.wait_ge(e_pnqk, m)
                dve.wait_ge(e_kl, m)
                nc.vector.tensor_tensor(heads(qkn[:, :], 8), heads(sl[:, 0:2 * D], 8),
                                        r8[:, 3, :].unsqueeze(2).to_broadcast([P, 8, HD]), ALU.mult).then_inc(e_qkn, 1)

            def prep_mean(m):
                dve.wait_ge(e_mm, m + 1)
                for h in range(2):
                    c = slice(h * HD, (h + 1) * HD)
                    ins = nc.vector.tensor_scalar(mmc[c, :], M1[c, h:NH:2], 1.0 / P, None, ALU.mult)
                ins.then_inc(e_mmc, 1)

            def lr_a(m):
                dve.wait_ge(e_z, m + 1)
                nc.vector.scalar_tensor_tensor(lt[:, 0, :], z[:, LR:MOM], -1.0, z[:, LR:MOM], ALU.mult, ALU.min).then_inc(e_lt, 1)

            def lr_b(m):
                dve.wait_ge(e_ex, m + 1)
                nc.vector.tensor_scalar(lt[:, 2, :], lt[:, 1, :], 1.0, None, ALU.add).then_inc(e_lt, 1)
                dve.wait_ge(e_lt, 3 * m + 2)
                nc.vector.tensor_scalar(lt[:, 4, :], lt[:, 2, :], -1.0, None, ALU.add)
                nc.vector.reciprocal(lt[:, 5, :], lt[:, 2, :]).then_inc(e_lt, 1)
                dve.wait_ge(e_lt, 3 * m + 3)
                nc.vector.tensor_tensor(lt[:, 6, :], lt[:, 1, :], lt[:, 4, :], ALU.subtract).then_inc(e_lr_steps, 1)
                dve.wait_ge(e_lr_steps, 3 * m + 1)
                nc.vector.tensor_tensor(lt[:, 6, :], lt[:, 6, :], lt[:, 5, :], ALU.mult).then_inc(e_lr_steps, 1)

            def lr_c(m):
                dve.wait_ge(e_ln, m + 1)
                nc.vector.scalar_tensor_tensor(lt[:, 7, :], z[:, LR:MOM], 0.0, lt[:, 3, :], ALU.max, ALU.add)\
                    .then_inc(e_lr_steps, 1)
                dve.wait_ge(e_lr_steps, 3 * m + 3)
                dve.wait_ge(e_kl, m)
                nc.vector.tensor_tensor(lr[:, :, :].rearrange("p h n -> p (h n)"), lt[:, 7, :], lt[:, 6, :], ALU.add)\
                    .then_inc(e_lr, 1)

            def k_side(i):
                tt, stt = nc.vector.tensor_tensor, nc.vector.scalar_tensor_tensor
                sg, hbm, dhi = ([ks[g][:, n, :] for g in range(G)] for n in range(3))

                def silu(g):
                    dve.wait_ge(e_kc[g], i + 1)
                    tt(kt[g][:, 0, :], CB[g][:, 0:P], sg[g], ALU.mult).then_inc(e_kd[g], 1)

                def slope(g):
                    dve.wait_ge(e_kd[g], 3 * i + 1)
                    stt(kt[g][:, 1, :], sg[g], 1.0, kt[g][:, 0, :], ALU.subtract, ALU.mult).then_inc(e_kd[g], 1)

                def derivative(g):
                    dve.wait_ge(e_kd[g], 3 * i + 2)
                    tt(kt[g][:, 2, :], sg[g], kt[g][:, 1, :], ALU.subtract).then_inc(e_kd[g], 1)

                def through(g):
                    dve.wait_ge(e_kd[g], 3 * i + 3)
                    dve.wait_ge(e_ku[g], i + 1)
                    tt(dga[g][:, :], kt[g][:, 2, :], kt[g][:, 3, :], ALU.mult).then_inc(e_dgr[g], 1)

                def hidden(g):
                    tt(hid[g][:, :], kt[g][:, 0, :], hbm[g], ALU.mult)

                def dhidden(g):
                    tt(dhb[g][:, :], kt[g][:, 0, :], dhi[g], ALU.mult)

                for step, g in ((silu, 0), (slope, 0), (hidden, 0), (silu, 1), (derivative, 0), (dhidden, 0), (slope, 1),
                                (through, 0), (hidden, 1), (derivative, 1), (dhidden, 1), (through, 1)):
                    step(g)

            def grad(i):
                flat = "p w c -> p (w c)"
                for g in range(G):
                    dve.wait_ge(e_dw[g], i + 1)
                    nc.vector.scalar_tensor_tensor(Mom[g][:, :, :].rearrange(flat), Mom[g][:, :, :].rearrange(flat),
                                                   mmc[:, g:g + 1], CA[g][:, 0:3 * HD], ALU.mult, ALU.add).then_inc(e_G[g], 1)
                for g in range(G):
                    dve.wait_ge(e_G[g], i + 1)
                    nc.vector.tensor_tensor(sq3[g][:, :, :], Mom[g][:, :, :], Mom[g][:, :, :], ALU.mult).then_inc(e_s3[g], 1)
                for g in range(G):
                    dve.wait_ge(e_s3[g], 2 * i + 1)
                    nc.vector.tensor_reduce(r3[g][:, 0, :], sq3[g][:, :, :], AX_X, ALU.add).then_inc(e_s3[g], 1)

            def sum_copy(i, g):
                dve.wait_ge(e_ssb[g], i + 1)
                nc.vector.tensor_copy(r3[g][:, 1, :], CB[g][:, 0:3]).then_inc(e_sst[g], 1)

            def x_first(i):
                for g in range(G):
                    dve.wait_ge(e_pw[g], i + 1)
                    nc.vector.tensor_scalar(r3[g][:, 2, :], r3[g][:, 2, :], 1e-7, None, ALU.add).then_inc(e_sst[g], 1)
                    dve.wait_ge(e_sst[g], 3 * i + 2)
                    nc.vector.reciprocal(r3[g][:, 1, :], r3[g][:, 2, :]).then_inc(e_sst[g], 1)
                    dve.wait_ge(e_sst[g], 3 * i + 3)
                    nc.vector.tensor_tensor(X[g][:, :, :], Mom[g][:, :, :],
                                            r3[g][:, 1, :].unsqueeze(2).to_broadcast([P, 3, HD]), ALU.mult).then_inc(e_x[g], 1)

            def ns_a(i, g, it):
                dve.wait_ge(e_prod[g], 3 * NI * i + 3 * it + 1)
                nc.vector.tensor_copy(Am[g][:, :, :].rearrange("p w c -> p (w c)"), CB[g][:, 0:3 * HD]).then_inc(e_am[g], 1)

            def ns_m(i, g, it):
                _, b, c = NS[it]
                dve.wait_ge(e_prod[g], 3 * NI * i + 3 * it + 2)
                nc.vector.scalar_tensor_tensor(Mp[g][:, :, :].rearrange("p w c -> p (w c)"),
                                               Am[g][:, :, :].rearrange("p w c -> p (w c)"), b / c, CA[g][:, 0:3 * HD],
                                               ALU.mult, ALU.add).then_inc(e_mp[g], 1)

            def ns_x(i, g, it):
                dve.wait_ge(e_prod[g], 3 * NI * i + 3 * it + 3)
                dve.wait_ge(e_ax[g], NI * i + it + 1)
                nc.vector.scalar_tensor_tensor(X[g][:, :, :].rearrange("p w c -> p (w c)"), CB[g][:, 0:3 * HD], NS[it][2],
                                               aX[g][:, :, :].rearrange("p w c -> p (w c)"), ALU.mult, ALU.add)\
                    .then_inc(e_x[g], 1)

            def row_sums(m):
                for g in range(G):
                    nc.vector.tensor_tensor(sq3[g][:, :, :], Wn[g][:, :, :], Wn[g][:, :, :], ALU.mult).then_inc(e_up[g], 1)
                for g in range(G):
                    dve.wait_ge(e_up[g], 4 * m + 1)
                    nc.vector.tensor_reduce(r3[g][:, 3, :], sq3[g][:, :, :], AX_X, ALU.add).then_inc(e_rn[g], 1)

            def update(i):
                for g in range(G):
                    dve.wait_ge(e_x[g], (NI + 1) * i + NI + 1)
                    nc.vector.tensor_tensor(Wn[g][:, :, :], Wn[g][:, :, :], X[g][:, :, :], ALU.add).then_inc(e_up[g], 1)
                for g in range(G):
                    dve.wait_ge(e_up[g], 4 * i + 4)
                row_sums(i + 1)

            def renorm(m):
                for g in range(G):
                    dve.wait_ge(e_rp[g], m + 1)
                    nc.vector.tensor_scalar(r3[g][:, 4, :], r3[g][:, 4, :], 1e-5, None, ALU.add).then_inc(e_up[g], 1)
                    dve.wait_ge(e_up[g], 4 * m + 2)
                    nc.vector.reciprocal(r3[g][:, 5, :], r3[g][:, 4, :]).then_inc(e_up[g], 1)
                    dve.wait_ge(e_up[g], 4 * m + 3)
                    nc.vector.tensor_tensor(r3[g][:, 5, :], r3[g][:, 5, :], nrm[g][:, :], ALU.mult).then_inc(e_rf[g], 1)
                    dve.wait_ge(e_rf[g], m)
                    nc.vector.tensor_tensor(Wn[g][:, :, :], Wn[g][:, :, :],
                                            r3[g][:, 5, :].unsqueeze(2).to_broadcast([P, 3, HD]), ALU.mult).then_inc(e_wn[g], 1)

            def q_gate(i):
                dve.wait_ge(e_gsig, i + 1)
                v = M0[:, :].rearrange("p (g w t) -> p g w t", g=G, w=2)
                nc.vector.tensor_tensor(gt1[:, :, :], v[:, :, 0, :], gsig[:, :, :], ALU.mult).then_inc(e_gt1, 1)
                dve.wait_ge(e_gt1, i + 1)
                nc.vector.tensor_tensor(gh[:, :, :], v[:, :, 1, :], gt1[:, :, :], ALU.mult).then_inc(e_gh, 1)

            def q_ms(i):
                dve.wait_ge(e_to, i + 1)
                nc.vector.tensor_reduce(r4[:, 0, :], heads(tsq[:, :], NH), AX_X, ALU.add).then_inc(e_msq, 1)
                dve.wait_ge(e_msq, 2 * i + 1)
                nc.vector.tensor_scalar(r4[:, 0, :], r4[:, 0, :], 1.0 / HD, 1e-5, ALU.mult, ALU.add).then_inc(e_msq, 1)

            def q_norm(i):
                nc.vector.tensor_tensor(r4[:, 2, :], z[:, SCL:GATE], sgs[:, SCL - MOM:GATE - MOM], ALU.mult).then_inc(e_tf, 1)
                dve.wait_ge(e_tf, 3 * i + 1)
                dve.wait_ge(e_rms, i + 1)
                nc.vector.tensor_tensor(r4[:, 3, :], r4[:, 2, :], r4[:, 1, :], ALU.mult).then_inc(e_tf, 1)
                dve.wait_ge(e_tf, 3 * i + 2)
                nc.vector.tensor_tensor(heads(tt1[:, :], NH), heads(to[:, :], NH),
                                        r4[:, 3, :].unsqueeze(2).to_broadcast([P, NH, HD]), ALU.mult).then_inc(e_tf, 1)
                dve.wait_ge(e_tf, 3 * i + 3)
                nc.vector.tensor_tensor(heads(ttt[:, :], NH), heads(tt1[:, :], NH),
                                        og_s[:, :].unsqueeze(1).to_broadcast([P, NH, HD]), ALU.mult).then_inc(e_ttt, 1)

            def att_scale(i):
                dve.wait_ge(e_at, i + 1)
                dve.wait_ge(e_win, 2 * i + 1)
                for c, dst in ((0, [aqT[:, h, :] for h in range(NAH)]), (1, [akT[:, h, 1, :] for h in range(NAH)])):
                    for h in range(NAH):
                        n = 2 * c + h
                        ins = nc.vector.tensor_scalar(dst[h], M1[:, n * P:(n + 1) * P], qks_s[:, h, c:c + 1],
                                                      qko_s[:, h, c:c + 1], ALU.mult, ALU.add)
                ins.then_inc(e_aT, 1)

            def att_mask(i):
                dve.wait_ge(e_as, i + 1)
                if not (isinstance(i, int) and i == 0):
                    dve.wait_ge(e_mask, 1)
                nc.vector.tensor_tensor(sm[:, :, :, :].rearrange("p h w k -> p h (w k)"), heads(M0[:, :], NAH),
                                        mask[:, :, :].rearrange("p w k -> p (w k)").unsqueeze(1)
                                        .to_broadcast([P, NAH, 2 * P]), ALU.add).then_inc(e_sm, 1)
                dve.wait_ge(e_sm, i + 1)
                nc.vector.tensor_reduce(r2[:, 0, :], sm[:, :, :, :].rearrange("p h w k -> p h (w k)"), AX_X, ALU.max)\
                    .then_inc(e_nmx, 1)
                dve.wait_ge(e_nmx, i + 1)
                nc.vector.tensor_scalar(r2[:, 1, :], r2[:, 0, :], -ATT_SCALE, None, ALU.mult).then_inc(e_nb, 1)

            def att_out(i):
                nc.vector.wait_ge(e_pr, i + 1)
                nc.vector.reciprocal(r2[:, 3, :], r2[:, 2, :]).then_inc(e_at2, 1)
                dve.wait_ge(e_at2, 2 * i + 1)
                dve.wait_ge(e_av, i + 1)
                nc.vector.tensor_tensor(heads(att[:, :], NAH), heads(M0[:, 0:D], NAH),
                                        r2[:, 3, :].unsqueeze(2).to_broadcast([P, NAH, P]), ALU.mult).then_inc(e_at2, 1)
                dve.wait_ge(e_at2, 2 * i + 2)
                dve.wait_ge(e_ttt, i + 1)
                nc.vector.tensor_tensor(comb[:, :], att[:, :], ttt[:, :], ALU.add).then_inc(e_comb, 1)

            def route(m):
                scores = sgs[:, GATE - MOM:SMALL - MOM]

                def biased():
                    dve.wait_ge(e_sgs, m + 1)
                    return nc.vector.tensor_tensor(sbias[:, :], scores, gb[:, :], ALU.add)

                def group_best():
                    for n in range(NG):
                        ins = nc.vector.max(g8[:, n, :], sbias[:, n * EPG:(n + 1) * EPG])
                    return ins

                def group_sum():
                    return nc.vector.tensor_tensor(gs[:, 0:NG], g8[:, :, 0], g8[:, :, 1], ALU.add)

                def groups_sorted():
                    return nc.vector.max(t8[:, :], gs[:, :])

                def groups_two():
                    return nc.vector.memset(t8[:, 2:8], NEG)

                def groups_marked():
                    return nc.vector.match_replace(gm[:, :], t8[:, :], gs[:, :], TAKEN)

                def penalty():
                    return nc.vector.tensor_scalar(pen[:, :], gm[:, 0:NG], TAKEN, 1.0, ALU.is_equal, ALU.subtract)

                def masked():
                    return nc.vector.scalar_tensor_tensor(
                        heads(msk[:, :], NG), pen[:, :].unsqueeze(2).to_broadcast([P, NG, EPG]), -NEG,
                        heads(sbias[:, :], NG), ALU.mult, ALU.add)

                def best():
                    return nc.vector.max(m8[:, :], msk[:, :])

                def best_marked():
                    return nc.vector.match_replace(mr[:, :], m8[:, :], msk[:, :], TAKEN)

                def selected():
                    return nc.vector.scalar_tensor_tensor(csel[:, :], mr[:, :], TAKEN, scores, ALU.is_equal, ALU.mult)

                def selected_sum():
                    return nc.vector.tensor_reduce(cs1[:, 0:1], csel[:, :], AX_X, ALU.add)

                def inverse():
                    return nc.vector.reciprocal(cs1[:, 1:2], cs1[:, 0:1])

                def after(step):
                    def run():
                        rt.wait()
                        step().then_inc(e_rt, 1)
                    return run

                rest = (group_best, group_sum, groups_sorted, groups_two, groups_marked, penalty, masked, best,
                        best_marked, selected, selected_sum, inverse)
                return [lambda: biased().then_inc(e_rt, 1)] + [after(step) for step in rest]

            def weights(m):
                rt.wait()
                dve.wait_ge(e_acc, NU * m)
                nc.vector.tensor_scalar(cw[:, :], csel[:, :], cs1[:, 1:2], ROUTED_SCALE, ALU.mult, ALU.mult).then_inc(e_cw, 1)

            def y_acc(i, u):
                dve.wait_ge(e_y, NU * i + u + 1)
                if u == 0:
                    dve.wait_ge(e_cw, i + 1)
                else:
                    dve.wait_ge(e_acc, NU * i + u)
                for e in range(EU):
                    w = cw[:, EU * u + e:EU * u + e + 1]
                    y = YB[:, e * P:(e + 1) * P]
                    if u == 0:
                        ins = nc.vector.tensor_scalar(acc[:, e, :], y, w, None, ALU.mult)
                    else:
                        ins = nc.vector.scalar_tensor_tensor(acc[:, e, :], y, w, acc[:, e, :], ALU.mult, ALU.add)
                ins.then_inc(e_acc, 1)

            def y_sum(i):
                dve.wait_ge(e_acc, NU * i + NU)
                nc.vector.tensor_tensor(ya[:, :, :], acc[:, 0:2, :], acc[:, 2:4, :], ALU.add).then_inc(e_ya, 1)
                dve.wait_ge(e_ya, i + 1)
                nc.vector.tensor_tensor(ys[:, :], ya[:, 0, :], ya[:, 1, :], ALU.add).then_inc(e_ys, 1)

            def total(i):
                dve.wait_ge(e_out, i + 1)
                dve.wait_ge(e_xr, 16 * i + 16)
                dve.wait_ge(e_stored, 16 * i)
                nc.vector.tensor_tensor(ot[:, :], M0[:, 0:D], xr[:, :], ALU.add).then_inc(e_ot, 1)

            def body(i, last):
                if last:
                    q_gate(i)
                    att_scale(i)
                    y_acc(i, 0)
                    q_ms(i)
                    att_mask(i)
                    y_acc(i, 1)
                    q_norm(i)
                    for u in range(2, NU):
                        y_acc(i, u)
                        if u == 3:
                            att_out(i)
                    y_sum(i)
                    total(i)
                    return
                m = i + 1
                k_side(i)
                q_gate(i)
                grad(i)
                sum_copy(i, 0)
                sum_copy(i, 1)
                ln_stats(m)
                x_first(i)
                routing = route(m)
                fill = {0: [lambda: y_acc(i, 0), lambda: ln_norm(m)], 1: [lambda: att_scale(i)], 2: [lambda: y_acc(i, 1)],
                        3: [lambda: q_ms(i)], 4: [lambda: y_acc(i, 2)],
                        5: [lambda: q_norm(i)], 7: [lambda: prep_silu_qk(m), lambda: prep_z(m)],
                        8: [lambda: prep_silu_v(m), lambda: prep_ss8(m)], 9: [lambda: y_acc(i, 3), lambda: prep_mean(m)],
                        10: [lambda: lr_a(m), lambda: prep_qkn(m)],
                        11: [lambda: att_mask(i)], 12: [lambda: y_acc(i, 4)], 13: [lambda: lr_b(m)],
                        14: [lambda: y_acc(i, 5), lambda: lr_c(m)], 16: [lambda: att_out(i)],
                        17: [lambda: y_acc(i, 6)], 18: [lambda: y_acc(i, 7)]}
                for st in range(4 * NI):
                    for g in range(G):
                        if st % 4:
                            (ns_a, ns_m, ns_x)[st % 4 - 1](i, g, st // 4)
                        if st > 10 and routing:
                            routing.pop(0)()
                    for f in fill.get(st, []):
                        f()
                update(i)
                y_sum(i)
                renorm(m)
                total(i)
                weights(m)

            dve.wait_ge(e_ttw, 16 * NTTW * G)
            row_sums(0)
            for g in range(G):
                dve.wait_ge(e_rp[g], 1)
                nc.vector.tensor_copy(nrm[g][:, :], r3[g][:, 4, :]).then_inc(e_up[g], 2)
            ln_stats(0)
            ln_norm(0)
            prep_z(0)
            prep_silu_qk(0)
            prep_silu_v(0)
            prep_ss8(0)
            prep_mean(0)
            prep_qkn(0)
            lr_a(0)
            lr_b(0)
            lr_c(0)
            for step in route(0):
                step()
            weights(0)
            body(0, False)
            with dve.Fori(1, LAST) as i:
                body(i, False)
            body(LAST, True)


def kernel(**inputs):
    import numpy as np
    import concourse.bacc as bacc
    from concourse.bass_utils import run_bass_kernel_spmd as run

    a = {k.replace("L0_", ""): np.asarray(v) for k, v in inputs.items()}
    q, k = np.arange(P)[:, None], np.arange(P)[None, :]
    masks = np.stack([np.full((P, P), NEG), np.where(k <= q, 0.0, NEG), np.where(k >= q, 0.0, NEG)], 1)
    arrays = {
        "x": a["attn_x"].reshape(-1, D), "wqkv": a["attn_Wqkv"], "wlr": a["attn_Wlr"], "wm": a["attn_Wm"],
        "bm": a["attn_bm"], "ws": a["attn_Ws"], "bs": a["attn_bs"], "wo": a["attn_Wo"],
        "w0": a["attn_w0"], "w1": a["attn_w1"], "w2": a["attn_w2"], "og": a["attn_o_norm_g"],
        "qks": a["attn_qk_scale"], "qko": a["attn_qk_offset"],
        "gateT": a["ffn_gate_w"].T, "gbias": a["ffn_gate_bias"], "fc1T": a["ffn_fc1_w"].T, "fc2T": a["ffn_fc2_w"].T,
        "e1T": a["ffn_w1"].transpose(2, 0, 1), "e2T": a["ffn_w2"].transpose(2, 0, 1),
        "upT": a["ffn_shared_up_w"].T, "downT": a["ffn_shared_down_w"].T,
        "ident": np.eye(P, dtype=np.float32), "bdones": np.kron(np.eye(2), np.ones((HD, HD))).astype(np.float32),
        "masks": masks.astype(np.float32),
    }
    arrays = {f"in_{n}": np.ascontiguousarray(v) for n, v in arrays.items()}
    nc = bacc.Bacc("TRN2", target_bir_lowering=False, num_devices=1)
    args = [nc.dram_tensor(n, v.shape, mybir.dt.from_np(v.dtype), kind="ExternalInput").ap() for n, v in arrays.items()]
    shape = arrays["in_x"].shape
    build(nc, *args, nc.dram_tensor("out_0", shape, F32, kind="ExternalOutput").ap())
    r = run(nc, [arrays], core_ids=[0])
    return r.results[0]["out_0"].reshape(1, *shape)
```

```python
import math
from contextlib import ExitStack

import concourse.bass as bass
from concourse import mybir

ALU = mybir.AluOpType
ACT = mybir.ActivationFunctionType
F32 = mybir.dt.float32
AX_X = mybir.AxisListType.X

P = 128
D = 256
KT = D // P
HD = 64
NH = 4
G = 2
AHD = 128
NAH = D // AHD
E = 32
NG = 4
EPG = E // NG
SH = 512
SC = SH // P
EU = 4
NU = E // EU
W0, W2, W1 = range(3)
BASE_LR = 0.01
LR_INV = BASE_LR + math.log(-math.expm1(-BASE_LR))
ATT_SCALE = AHD ** -0.5
ROUTED_SCALE = 2.5
NEG = -1e30
TAKEN = -2e30
NS = [(4.0848, -6.8946, 2.927), (3.9505, -6.3029, 2.6377), (3.7418, -5.5913, 2.3037),
      (2.8769, -3.1427, 1.2046), (2.8366, -3.0525, 1.2012)]
NI = len(NS)
LR, MOM, SCL, GATE, SMALL = 0, 12, 16, 20, 52


class Expect:

    def __init__(self, eng, sem, name, first=1, step=1):
        self.eng, self.sem, self.step = eng, sem, step
        self.reg = eng.alloc_register(name)
        eng.reg_mov(self.reg, first)

    def wait(self, skip=0):
        self.eng.wait_ge(self.sem, self.reg)
        self.eng.reg_add(self.reg, self.reg, self.step + skip)


def build(nc, x, wall_d, rows_d, wo, fast_d, affine_d, fc1T, fc2T, e1T, e2T, upT, downT, ident_d, fixed_d, out):
    T = x.shape[0]
    NT = T // P
    LAST = NT - 1
    with ExitStack() as ctx:
        def sb(name, shape):
            return ctx.enter_context(nc.sbuf_tensor(name, shape, F32))

        def bank(name):
            return ctx.enter_context(nc.psum_tensor(name, [P, 512], F32))

        def sem(name):
            return ctx.enter_context(nc.semaphore(name))

        wall = sb("wall", [P, KT, 3 * D + SMALL])
        wo_s = sb("wo_s", [P, KT, D])
        fc1_s = sb("fc1_s", [P, KT, P])
        fc2_s = sb("fc2_s", [P, D])
        up_s = sb("up_s", [P, KT, SH])
        down_s = sb("down_s", [P, SC, D])
        e1_s = sb("e1_s", [P, E, P])
        e2_s = sb("e2_s", [P, E, P])
        ident = sb("ident", [P, P])
        fixed = sb("fixed", [P, 4, P])
        ones = sb("ones", [P, P])
        rows = sb("rows", [P, SMALL + E + HD])
        affine = sb("affine", [P, NAH, 4])
        half = sb("half", [P, 8])
        neghalf = sb("neghalf", [P, 8])
        a_tile = sb("a_tile", [P, NI, 3 * HD])
        bdones, mask, mask_prev = fixed[:, 0, :], fixed[:, 1:3, :], fixed[:, 3, :]
        bias, gb, og_s = rows[:, 0:SMALL], rows[:, SMALL:SMALL + E], rows[:, SMALL + E:SMALL + E + HD]
        Wn = [sb(f"Wn{g}", [P, 3, HD]) for g in range(G)]
        W1BD = [sb(f"W1BD{g}", [P, P]) for g in range(G)]
        WT = [sb(f"WT{g}", [P, 3, P]) for g in range(G)]
        Mom = [sb(f"Mom{g}", [P, 3, HD]) for g in range(G)]
        nrm = [sb(f"nrm{g}", [P, 3]) for g in range(G)]
        X = [sb(f"X{g}", [P, 3, HD]) for g in range(G)]
        aX = [sb(f"aX{g}", [P, 3, HD]) for g in range(G)]
        XT = [sb(f"XT{g}", [HD, 3, P]) for g in range(G)]
        Am = [sb(f"Am{g}", [P, 3, HD]) for g in range(G)]
        Mp = [sb(f"Mp{g}", [P, 3, HD]) for g in range(G)]
        sq3 = [sb(f"sq3{g}", [P, 3, HD]) for g in range(G)]
        r3 = [sb(f"r3{g}", [P, 6, 3]) for g in range(G)]
        ks = [sb(f"ks{g}", [P, 3, P]) for g in range(G)]
        kt = [sb(f"kt{g}", [P, 4, P]) for g in range(G)]
        dga = [sb(f"dga{g}", [P, P]) for g in range(G)]
        dhb = [sb(f"dhb{g}", [P, P]) for g in range(G)]
        hid = [sb(f"hid{g}", [P, P]) for g in range(G)]
        xa = sb("xa", [P, D])
        xr = sb("xr", [P, D])
        ot = sb("ot", [P, D])
        st6 = sb("st6", [P, 6])
        mv = sb("mv", [P, 2])
        rstd = sb("rstd", [P, 2])
        xn = sb("xn", [P, D])
        xnT = sb("xnT", [P, KT, P])
        raw = sb("raw", [P, 3 * D])
        sig = sb("sig", [P, 3 * D])
        sl = sb("sl", [P, 3 * D])
        sq8 = sb("sq8", [P, 2 * D])
        r8 = sb("r8", [P, 4, 8])
        qkn = sb("qkn", [P, 2 * D])
        z = sb("z", [P, SMALL])
        sgs = sb("sgs", [P, SMALL - MOM])
        lt = sb("lt", [P, 8, 12])
        lr = sb("lr", [P, NH, 3])
        kl0 = sb("kl0", [P, NH, HD])
        kl2 = sb("kl2", [P, NH, HD])
        vl1 = sb("vl1", [P, NH, HD])
        mmc = sb("mmc", [P, G])
        qkT = sb("qkT", [P, 4, P])
        vT = sb("vT", [P, G, P])
        gsig = sb("gsig", [P, G, P])
        gt1 = sb("gt1", [P, G, P])
        gh = sb("gh", [P, G, P])
        to = sb("to", [P, D])
        tsq = sb("tsq", [P, D])
        r4 = sb("r4", [P, 4, 4])
        tt1 = sb("tt1", [P, D])
        ttt = sb("ttt", [P, D])
        aqT = sb("aqT", [P, NAH, P])
        akT = sb("akT", [P, NAH, 2, P])
        vw = sb("vw", [P, 2, D])
        sm = sb("sm", [P, NAH, 2, P])
        pr = sb("pr", [P, NAH, 2, P])
        prT = sb("prT", [P, NAH, 2, P])
        r2 = sb("r2", [P, 4, 2])
        att = sb("att", [P, D])
        comb = sb("comb", [P, D])
        combT = sb("combT", [P, KT, P])
        sbias = sb("sbias", [P, E])
        g8 = sb("g8", [P, NG, 8])
        gs = sb("gs", [P, 12])
        t8 = sb("t8", [P, 8])
        gm = sb("gm", [P, 12])
        pen = sb("pen", [P, NG])
        msk = sb("msk", [P, E])
        m8 = sb("m8", [P, 8])
        mr = sb("mr", [P, E])
        csel = sb("csel", [P, E])
        cs1 = sb("cs1", [P, 2])
        cw = sb("cw", [P, E])
        xlT = sb("xlT", [P, P])
        ur = sb("ur", [P, SC, P])
        us = sb("us", [P, SC, P])
        hr = [sb(f"hr{b}", [P, EU, P]) for b in range(2)]
        hq = [sb(f"hq{b}", [P, EU, P]) for b in range(2)]
        acc = sb("acc", [P, EU, P])
        ya = sb("ya", [P, 2, P])
        ys = sb("ys", [P, P])
        yT = sb("yT", [P, P])

        CA = [bank(f"CA{g}") for g in range(G)]
        CB = [bank(f"CB{g}") for g in range(G)]
        M0 = bank("M0")
        M1 = bank("M1")
        HB = bank("HB")
        YB = bank("YB")

        def per_group(name):
            return [sem(f"{name}{g}") for g in range(G)]

        e_ident = sem("ident_in")
        e_const, e_later, e_up_w, e_down_w, e_ttw, e_init = (sem(n) for n in (
            "first_const_in", "later_const_in", "up_weights_in", "down_weights_in", "fast_weights_in", "init"))
        e_xa, e_xr, e_stored = sem("xa_in"), sem("xr_in"), sem("stored")
        e_stats, e_aggr, e_veps, e_rstd, e_xn = (sem(n) for n in ("stats", "aggr", "veps", "rstd", "xn_ready"))
        e_pt, e_xnT, e_pqa, e_pqb = (sem(n) for n in ("xn_turned", "xnT_ready", "qk_projected", "v_projected"))
        e_rawqk, e_rawv, e_z, e_sgs = (sem(n) for n in ("raw_qk", "raw_v", "z_ready", "sigmoids"))
        e_slqk, e_slv, e_sq8, e_ss8, e_n8, e_r8 = (sem(n) for n in ("silu_qk", "silu_v", "sq8", "ss8", "n8", "r8"))
        e_qkn, e_mm, e_mmc = (sem(n) for n in ("qkn_ready", "mom_summed", "mom_mean"))
        e_pnv, e_pnqk, e_vT, e_qkT = (sem(n) for n in ("v_turned", "qkn_turned", "vT_ready", "qkT_ready"))
        e_lt, e_ex, e_ln, e_lr, e_kl = (sem(n) for n in ("lr_steps", "lr_exp", "lr_ln", "lr_ready", "kl_ready"))
        e_k, e_kc, e_kd, e_ku, e_dgr = (per_group(n) for n in ("k_side", "k_copied", "k_steps", "k_u", "dgba"))
        e_dw, e_G, e_s3, e_ssb, e_sst, e_pw, e_x = (per_group(n) for n in ("dw", "G", "s3", "ssb", "sst", "pw", "X"))
        e_ax, e_t, e_xt, e_am = (per_group(n) for n in ("aX", "turn", "XT", "Am"))
        e_prod, e_mp = (per_group(n) for n in ("product", "Mp"))
        e_up, e_rn, e_rp, e_wn, e_bd, e_wt, e_WT = (per_group(n) for n in ("upd", "rn", "rp", "Wn", "W1BD", "wt", "WT"))
        e_qs, e_gsig, e_gt1, e_gh, e_qo, e_to = (sem(n) for n in ("q_side", "gate_sig", "gt1", "gh", "q_out", "to_copied"))
        e_msq, e_rms, e_tf, e_ttt = (sem(n) for n in ("ms", "rms", "ttt_steps", "ttt_ready"))
        e_at, e_aT, e_win, e_as, e_sm, e_nb, e_pr = (sem(n) for n in ("raw_turned", "aT", "window", "scores", "masked", "negmax", "probs"))
        e_ap, e_prT, e_av, e_at2, e_comb, e_ct, e_combT = (sem(n) for n in ("probs_turned", "prT", "att_pv", "att_steps", "comb", "comb_turned", "combT"))
        e_mask = sem("mask_ready")
        e_rt, e_cw = sem("route_steps"), sem("cw_ready")
        e_lr_steps, e_nmx = sem("lr_sum_steps"), sem("max_ready")
        e_fx, e_xlT, e_upm, e_ur, e_us = (sem(n) for n in ("fc1", "xlT", "shared_up", "shared_relu", "shared_sq"))
        e_h, e_hr, e_hq, e_y, e_acc = (sem(n) for n in ("h", "h_relu", "h_sq", "y", "acc"))
        e_ya, e_ys, e_yt, e_yT, e_out, e_ot = (sem(n) for n in ("ya", "y_sum", "y_turned", "yT", "out_mm", "out_ready"))

        NCONST, NLATER, NUP, NDOWN = 2, 3, 3, 3

        block = ctx.enter_context(nc.Block())

        @block.sync
        def _(sp):
            sp.dma_start(xa[:, :], x[0:P, :]).then_inc(e_xa, 16)
            sp.dma_start(ident[:, :], ident_d[:, :]).then_inc(e_ident, 16)
            for dst, src in ((wall[:, :, :], wall_d[:, :, :]),
                             (rows[:, :], rows_d.partition_broadcast(P))):
                sp.dma_start(dst, src).then_inc(e_const, 16)
            for dst, src in ((fixed[:, :, :], fixed_d[:, :, :]), (affine[:, :, :], affine_d[:, :, :]),
                             (wo_s[:, :, :], wo.rearrange("(k p) n -> p k n", p=P))):
                sp.dma_start(dst, src).then_inc(e_later, 16)
            sp.wait_ge(e_xn, 1)
            sp.dma_start(xa[:, :], x[P:2 * P, :]).then_inc(e_xa, 16)
            sp.dma_start(xr[:, :], x[0:P, :]).then_inc(e_xr, 16)

            def store(i, rows):
                sp.wait_ge(e_ot, i + 1)
                sp.dma_start(out[bass.ds(rows, P), :], ot[:, :]).then_inc(e_stored, 16)

            with sp.Fori(0, NT - 2) as i:
                here, after, later = sp.snap(i * P), sp.snap((i + 1) * P), sp.snap((i + 2) * P)
                sp.wait_ge(e_xn, i + 2)
                sp.dma_start(xa[:, :], x[bass.ds(later, P), :]).then_inc(e_xa, 16)
                store(i, here)
                sp.dma_start(xr[:, :], x[bass.ds(after, P), :]).then_inc(e_xr, 16)
            store(NT - 2, (NT - 2) * P)
            sp.dma_start(xr[:, :], x[LAST * P:T, :]).then_inc(e_xr, 16)
            store(LAST, LAST * P)
            sp.wait_ge(e_stored, 16 * NT)

        @block.gpsimd
        def _(pool):
            win_scores = Expect(pool, e_as, "win_scores", first=2)
            win_pv = Expect(pool, e_av, "win_pv", first=2)
            win_raw = Expect(pool, e_rawv, "win_raw", first=3)
            win_vw = Expect(pool, e_win, "win_vw", first=5, step=2)
            pool.wait_ge(e_init, 1)

            def power(dst, src, expo, n):
                return pool.tensor_tensor(dst, src, expo[:, 0:n], ALU.pow)

            def prep_rstd(m):
                pool.wait_ge(e_veps, m + 1)
                power(rstd[:, 0:1], rstd[:, 1:2], neghalf, 1).then_inc(e_rstd, 1)

            def prep_n8(m):
                pool.wait_ge(e_ss8, m + 1)
                power(r8[:, 1, :], r8[:, 0, :], half, 8).then_inc(e_n8, 1)

            def prep_kl(m):
                pool.wait_ge(e_lr, m + 1)
                for g in range(G):
                    pool.wait_ge(e_dw[g], m)
                kk = qkn[:, D:2 * D].rearrange("p (h c) -> p h c", c=HD)
                vv = sl[:, 2 * D:3 * D].rearrange("p (h c) -> p h c", c=HD)
                for dst, src, n in ((kl0, kk, 0), (kl2, kk, 2), (vl1, vv, 1)):
                    ins = pool.tensor_tensor(dst[:, :, :], src, lr[:, :, n:n + 1].to_broadcast([P, NH, HD]), ALU.mult)
                ins.then_inc(e_kl, 1)

            def window(m, known):
                if known:
                    pool.wait_ge(e_as, m)
                    pool.wait_ge(e_av, m)
                    pool.wait_ge(e_rawv, m + 1)
                else:
                    win_scores.wait()
                    win_pv.wait()
                    win_raw.wait()
                pool.tensor_copy(akT[:, :, 0, :], akT[:, :, 1, :])
                pool.tensor_copy(vw[:, 0, :], vw[:, 1, :]).then_inc(e_win, 1)
                if known:
                    pool.wait_ge(e_win, 2 * m + 1)
                else:
                    win_vw.wait()
                pool.tensor_copy(vw[:, 1, :], raw[:, 2 * D:3 * D]).then_inc(e_win, 1)

            def restore_mask():
                pool.wait_ge(e_sm, 1)
                pool.wait_ge(e_later, 16 * NLATER)
                pool.tensor_copy(mask[:, 0, :], mask_prev[:, :]).then_inc(e_mask, 1)

            def k_u(i, g):
                pool.wait_ge(e_kc[g], i + 1)
                pool.tensor_tensor(kt[g][:, 3, :], ks[g][:, 1, :], ks[g][:, 2, :], ALU.mult).then_inc(e_ku[g], 1)

            def ss_pow(i, g):
                pool.wait_ge(e_sst[g], 3 * i + 1)
                power(r3[g][:, 2, :], r3[g][:, 1, :], half, 3).then_inc(e_pw[g], 1)

            def ax(i, g, it):
                pool.wait_ge(e_x[g], (NI + 1) * i + it + 1)
                pool.tensor_tensor(aX[g][:, :, :].rearrange("p w c -> p (w c)"),
                                   X[g][:, :, :].rearrange("p w c -> p (w c)"), a_tile[:, it, :],
                                   ALU.mult).then_inc(e_ax[g], 1)

            def row_pow(m, g):
                pool.wait_ge(e_rn[g], m + 1)
                power(r3[g][:, 4, :], r3[g][:, 3, :], half, 3).then_inc(e_rp[g], 1)

            def rms_pow(i):
                pool.wait_ge(e_msq, 2 * i + 2)
                power(r4[:, 1, :], r4[:, 0, :], neghalf, 4).then_inc(e_rms, 1)

            def shared_sq(i):
                pool.wait_ge(e_ur, i + 1)
                pool.tensor_tensor(us[:, :, :], ur[:, :, :], ur[:, :, :], ALU.mult).then_inc(e_us, 1)

            def h_sq(i, u):
                pool.wait_ge(e_hr, NU * i + u + 1)
                if u > 1 or not (isinstance(i, int) and i == 0):
                    pool.wait_ge(e_y, NU * i + u - 1)
                b = u % 2
                pool.tensor_tensor(hq[b][:, :, :], hr[b][:, :, :], hr[b][:, :, :], ALU.mult).then_inc(e_hq, 1)

            def body(i, last):
                if last:
                    h_sq(i, 1)
                    h_sq(i, 2)
                    shared_sq(i)
                    h_sq(i, 3)
                    rms_pow(i)
                    for u in range(4, NU):
                        h_sq(i, u)
                    return
                m = i + 1
                first = isinstance(i, int)
                k_u(i, 0)
                k_u(i, 1)
                h_sq(i, 1)
                for g in range(G):
                    ss_pow(i, g)
                prep_rstd(m)
                h_sq(i, 2)
                fill = {0: [lambda: shared_sq(i)], 1: [lambda: h_sq(i, 3)], 3: [lambda: rms_pow(i)],
                        4: [lambda: h_sq(i, 4)], 9: [lambda: prep_n8(m), lambda: h_sq(i, 5)],
                        12: [lambda: h_sq(i, 6)], 14: [lambda: h_sq(i, 7)], 16: [lambda: window(m, first)],
                        17: [lambda: prep_kl(m)]}
                if first:
                    fill[13] = [restore_mask]
                for st in range(4 * NI):
                    if st % 4 == 0:
                        for g in range(G):
                            ax(i, g, st // 4)
                    for f in fill.get(st, []):
                        f()
                for g in range(G):
                    row_pow(m, g)
                h_sq(m, 0)

            prep_rstd(0)
            for g in range(G):
                row_pow(0, g)
            prep_n8(0)
            window(0, True)
            prep_kl(0)
            h_sq(0, 0)
            body(0, False)
            with pool.Fori(1, LAST) as i:
                body(i, False)
            body(LAST, True)

        @block.scalar
        def _(act):
            for g in range(G):
                act.dma_start(Wn[g][:, :, :], fast_d[g]).then_inc(e_ttw, 16)
            for dst, src in ((fc1_s[:, :, :], fc1T.rearrange("(k p) n -> p k n", p=P)), (e1_s[:, :, :], e1T),
                             (up_s[:, :, :], upT.rearrange("(k p) n -> p k n", p=P))):
                act.dma_start(dst, src).then_inc(e_up_w, 16)
            for dst, src in ((e2_s[:, :, :], e2T), (down_s[:, :, :], downT.rearrange("(k p) n -> p k n", p=P)),
                             (fc2_s[:, :], fc2T)):
                act.dma_start(dst, src).then_inc(e_down_w, 16)

            def a(out_, in_, func, **kw):
                return nc.scalar.activation(out_, in_, func, **kw)

            def prep_xnT(m):
                act.wait_ge(e_pt, m + 1)
                a(xnT[:, :, :].rearrange("p k t -> p (k t)"), M0[:, 0:D], ACT.Copy).then_inc(e_xnT, 1)

            def prep_qk(m):
                act.wait_ge(e_pqa, m + 1)
                act.wait_ge(e_at, m)
                act.wait_ge(e_slv, m)
                a(sig[:, 0:2 * D], M0[:, :], ACT.Sigmoid)
                a(raw[:, 0:2 * D], M0[:, :], ACT.Copy).then_inc(e_rawqk, 1)

            def prep_v(m):
                act.wait_ge(e_pqb, m + 1)
                act.wait_ge(e_win, 2 * m)
                a(sig[:, 2 * D:3 * D], M1[:, 0:D], ACT.Sigmoid)
                a(raw[:, 2 * D:3 * D], M1[:, 0:D], ACT.Copy).then_inc(e_rawv, 1)

            def prep_small(m):
                act.wait_ge(e_z, m + 1)
                act.wait_ge(e_cw, m)
                act.wait_ge(e_ttt, m)
                a(sgs[:, :], z[:, MOM:SMALL], ACT.Sigmoid).then_inc(e_sgs, 1)

            def prep_sq8(m):
                act.wait_ge(e_slqk, m + 1)
                a(sq8[:, :], sl[:, 0:2 * D], ACT.Square).then_inc(e_sq8, 1)

            def prep_vT(m):
                act.wait_ge(e_pnv, m + 1)
                a(vT[:, :, :].rearrange("p g t -> p (g t)"), M0[:, 0:D], ACT.Copy).then_inc(e_vT, 1)

            def prep_qkT(m):
                act.wait_ge(e_pnqk, m + 1)
                a(qkT[:, :, :].rearrange("p g t -> p (g t)"), M1[:, :], ACT.Copy).then_inc(e_qkT, 1)

            def lr_exp(m):
                act.wait_ge(e_lt, 3 * m + 1)
                a(lt[:, 1, :], lt[:, 0, :], ACT.Exp).then_inc(e_ex, 1)

            def lr_ln(m):
                act.wait_ge(e_lt, 3 * m + 2)
                a(lt[:, 3, :], lt[:, 2, :], ACT.Ln).then_inc(e_ln, 1)

            def k_side(i, g):
                act.wait_ge(e_k[g], i + 1)
                a(ks[g][:, 0, :], CB[g][:, 0:P], ACT.Sigmoid)
                a(ks[g][:, 1:3, :].rearrange("p w c -> p (w c)"), CB[g][:, P:3 * P], ACT.Copy).then_inc(e_kc[g], 1)

            def xt(i, g, it):
                act.wait_ge(e_t[g], NI * i + it + 1)
                a(XT[g][:, :, :].rearrange("p w c -> p (w c)"), CA[g][0:HD, 0:3 * P], ACT.Copy).then_inc(e_xt[g], 1)

            def w_T(m, g):
                act.wait_ge(e_wt[g], m + 1)
                for h in range(2):
                    c = slice(h * HD, (h + 1) * HD)
                    ins = a(WT[g][c, :, c], CA[g][0:HD, 0:3 * P].rearrange("p (w c) -> p w c", w=3)[:, :, c], ACT.Copy)
                ins.then_inc(e_WT[g], 1)

            def gate_sig(i):
                act.wait_ge(e_qs, i + 1)
                a(gsig[:, :, :], M0[:, :].rearrange("p (g w t) -> p g w t", g=G, w=2)[:, :, 0, :], ACT.Sigmoid)\
                    .then_inc(e_gsig, 1)

            def q_out(i):
                act.wait_ge(e_qo, i + 1)
                a(to[:, :], M1[:, 0:D], ACT.Copy)
                a(tsq[:, :], M1[:, 0:D], ACT.Square).then_inc(e_to, 1)

            def x_lat(m):
                act.wait_ge(e_fx, m + 1)
                act.wait_ge(e_h, NU * m)
                a(xlT[:, :], M1[:, 0:P], ACT.Copy).then_inc(e_xlT, 1)

            def shared_relu(i):
                act.wait_ge(e_upm, i + 1)
                a(ur[:, :, :].rearrange("p s t -> p (s t)"), M0[:, :], ACT.Relu).then_inc(e_ur, 1)

            def h_relu(i, u):
                act.wait_ge(e_h, NU * i + u + 1)
                if u > 1 or not (isinstance(i, int) and i == 0):
                    act.wait_ge(e_hq, NU * i + u - 1)
                a(hr[u % 2][:, :, :].rearrange("p s t -> p (s t)"), HB[:, :], ACT.Relu).then_inc(e_hr, 1)

            def y_first(i):
                act.wait_ge(e_y, NU * i + 1)
                act.wait_ge(e_cw, i + 1)
                act.wait_ge(e_ys, i)
                for e in range(EU):
                    ins = a(acc[:, e, :], YB[:, e * P:(e + 1) * P], ACT.Copy, scale=cw[:, e:e + 1])
                ins.then_inc(e_acc, 1)

            def probs(i):
                act.wait_ge(e_nb, i + 1)
                for h in range(NAH):
                    ins = a(pr[:, h].rearrange("p w k -> p (w k)"), sm[:, h].rearrange("p w k -> p (w k)"), ACT.Exp,
                            bias=r2[:, 1, h:h + 1], scale=ATT_SCALE, accum_out=r2[:, 2, h:h + 1])
                ins.then_inc(e_pr, 1)

            def probs_T(i):
                act.wait_ge(e_ap, i + 1)
                a(prT[:, :, :, :].rearrange("p h w k -> p (h w k)"), M1[:, :], ACT.Copy).then_inc(e_prT, 1)

            def comb_T(i):
                act.wait_ge(e_ct, i + 1)
                a(combT[:, :, :].rearrange("p h k -> p (h k)"), M1[:, 0:D], ACT.Copy).then_inc(e_combT, 1)

            def y_T(i):
                act.wait_ge(e_yt, i + 1)
                a(yT[:, :], M1[:, 0:P], ACT.Copy).then_inc(e_yT, 1)

            def body(i, last):
                if last:
                    gate_sig(i)
                    y_first(i)
                    h_relu(i, 2)
                    shared_relu(i)
                    h_relu(i, 3)
                    q_out(i)
                    act.preload_act_table_set("natural_log_exp_and_others")
                    h_relu(i, 4)
                    probs(i)
                    h_relu(i, 5)
                    probs_T(i)
                    h_relu(i, 6)
                    h_relu(i, 7)
                    comb_T(i)
                    y_T(i)
                    return
                m = i + 1
                k_side(i, 0)
                k_side(i, 1)
                gate_sig(i)
                y_first(i)
                h_relu(i, 2)

                def to_exp():
                    act.preload_act_table_set("natural_log_exp_and_others")

                def to_sigmoid():
                    act.preload_act_table_set("sigmoid_and_others")

                shared_relu(i)
                h_relu(i, 3)
                fill = {1: [lambda: h_relu(i, 4)], 2: [lambda: q_out(i), lambda: prep_xnT(m)],
                        5: [lambda: prep_qk(m)], 6: [lambda: prep_v(m)], 7: [lambda: h_relu(i, 5), lambda: prep_small(m)],
                        8: [lambda: prep_sq8(m)], 9: [lambda: prep_vT(m), lambda: h_relu(i, 6), to_exp],
                        11: [lambda: lr_exp(m)], 12: [lambda: prep_qkT(m)],
                        13: [lambda: probs(i)], 14: [lambda: h_relu(i, 7), lambda: lr_ln(m)], 15: [lambda: probs_T(i), to_sigmoid],
                        18: [lambda: comb_T(i)], 19: [lambda: x_lat(m)]}
                for st in range(4 * NI):
                    if st % 4 == 0:
                        for g in range(G):
                            xt(i, g, st // 4)
                    for f in fill.get(st, []):
                        f()
                h_relu(m, 0)
                y_T(i)
                h_relu(m, 1)
                for g in range(G):
                    w_T(m, g)

            act.preload_act_table_set("sigmoid_and_others")
            act.wait_ge(e_init, 2)
            prep_xnT(0)
            prep_qk(0)
            prep_v(0)
            prep_small(0)
            prep_sq8(0)
            for g in range(G):
                w_T(0, g)
            prep_vT(0)
            x_lat(0)
            act.preload_act_table_set("natural_log_exp_and_others")
            lr_exp(0)
            h_relu(0, 0)
            prep_qkT(0)
            lr_ln(0)
            act.preload_act_table_set("sigmoid_and_others")
            h_relu(0, 1)
            body(0, False)
            with act.Fori(1, LAST) as i:
                body(i, False)
            body(LAST, True)

        @block.tensor
        def _(pe):
            x_turn = [Expect(pe, e_x[g], f"x_turn{g}") for g in range(G)]
            xt_in = [Expect(pe, e_xt[g], f"xt_in{g}") for g in range(G)]
            am_in = [Expect(pe, e_am[g], f"am_in{g}") for g in range(G)]
            mp_in = [Expect(pe, e_mp[g], f"mp_in{g}") for g in range(G)]
            d_in = [Expect(pe, e_dgr[g], f"d_in{g}") for g in range(G)]
            wn_in = [Expect(pe, e_wn[g], f"wn_in{g}", first=2) for g in range(G)]
            kl_in = Expect(pe, e_kl, "kl_in")
            pe.wait_ge(e_ident, 16)
            pe.wait_ge(e_init, 2)

            def mm(out_, lhsT, rhs, start=True, stop=True):
                return pe.matmul(out_, lhsT, rhs, start=start, stop=stop)

            def prep_turn(m):
                pe.wait_ge(e_xn, m + 1)
                pe.wait_ge(e_ur, m)
                for k in range(KT):
                    ins = pe.transpose(M0[:, k * P:(k + 1) * P], xn[:, k * P:(k + 1) * P], ident[:, :])
                ins.then_inc(e_pt, 1)

            def prep_qk(m):
                pe.wait_ge(e_xnT, m + 1)
                mm(M0[:, :], xnT[:, 0, :], wall[:, 0, 0:2 * D], True, False)

            def prep_qk_more(m):
                for k in range(1, KT):
                    ins = mm(M0[:, :], xnT[:, k, :], wall[:, k, 0:2 * D], False, k == KT - 1)
                ins.then_inc(e_pqa, 1)

            def prep_v(m):
                pe.wait_ge(e_to, m)
                for k in range(KT):
                    ins = mm(M1[:, 0:D + SMALL], xnT[:, k, :], wall[:, k, 2 * D:3 * D + SMALL], k == 0, k == KT - 1)
                ins.then_inc(e_pqb, 1)

            def prep_mom(m):
                pe.wait_ge(e_sgs, m + 1)
                mm(M1[:, 0:NH], ones[:, :], sgs[:, 0:NH]).then_inc(e_mm, 1)

            def prep_turn_v(m):
                pe.wait_ge(e_slv, m + 1)
                pe.wait_ge(e_rawqk, m + 1)
                for g in range(G):
                    ins = pe.transpose(M0[:, g * P:(g + 1) * P], sl[:, 2 * D + g * P:2 * D + (g + 1) * P], ident[:, :])
                ins.then_inc(e_pnv, 1)

            def prep_turn_qk(m):
                pe.wait_ge(e_qkn, m + 1)
                pe.wait_ge(e_mmc, m + 1)
                for n in range(4):
                    ins = pe.transpose(M1[:, n * P:(n + 1) * P], qkn[:, n * P:(n + 1) * P], ident[:, :])
                ins.then_inc(e_pnqk, 1)

            def k_side(i, g):
                pe.wait_ge(e_qkT, i + 1)
                pe.wait_ge(e_vT, i + 1)
                pe.wait_ge(e_WT[g], i + 1)
                mm(CB[g][:, 0:2 * P], qkT[:, 2 + g, :], WT[g][:, W0:W2 + 1, :].rearrange("p w c -> p (w c)"))
                pe.wait_ge(e_bd[g], i + 1)
                mm(CB[g][:, 2 * P:3 * P], vT[:, g, :], W1BD[g][:, :]).then_inc(e_k[g], 1)

            def grads(i, g):
                if g == 0:
                    kl_in.wait()
                d_in[g].wait()
                for h in range(2):
                    c = slice(h * HD, (h + 1) * HD)
                    mm(CA[g][c, 0:HD], dga[g][:, c], kl0[:, 2 * g + h, :])
                    mm(CA[g][c, HD:2 * HD], dhb[g][:, c], kl2[:, 2 * g + h, :])
                    ins = mm(CA[g][c, 2 * HD:3 * HD], vl1[:, 2 * g + h, :], hid[g][:, c])
                ins.then_inc(e_dw[g], 1)

            def sums(i, g):
                pe.wait_ge(e_s3[g], 2 * i + 2)
                mm(CB[g][:, 0:3], bdones[:, :], r3[g][:, 0, :]).then_inc(e_ssb[g], 1)

            def ns_turn(g, last_step):
                x_turn[g].wait(skip=1 if last_step else 0)
                for w in range(3):
                    ins = pe.transpose(CA[g][0:HD, w * P:(w + 1) * P], X[g][:, w, :], ident[:, :])
                ins.then_inc(e_t[g], 1)

            def ns_gram(g):
                xt_in[g].wait()
                for w in range(3):
                    for h in range(2):
                        c = slice(h * HD, (h + 1) * HD)
                        ins = mm(CB[g][c, w * HD:(w + 1) * HD], XT[g][:, w, c], XT[g][:, w, c])
                ins.then_inc(e_prod[g], 1)

            def ns_pair(g, bank_, ready, left, right):
                ready[g].wait()
                for w in range(3):
                    for h in range(2):
                        c = slice(h * HD, (h + 1) * HD)
                        ins = mm(bank_[g][c, w * HD:(w + 1) * HD], left[g][c, w, :], right[g][c, w, :])
                ins.then_inc(e_prod[g], 1)

            def turn_w(m, g):
                if isinstance(m, int):
                    if m == 0:
                        pe.wait_ge(e_ttw, 16 * G)
                    else:
                        pe.wait_ge(e_wn[g], m)
                else:
                    wn_in[g].wait()
                for w in range(3):
                    ins = pe.transpose(CA[g][0:HD, w * P:(w + 1) * P], Wn[g][:, w, :], ident[:, :])
                ins.then_inc(e_wt[g], 1)

            def q_side(i):
                pe.wait_ge(e_ot, i)
                for g in range(G):
                    pe.wait_ge(e_WT[g], i + 1)
                pe.wait_ge(e_qkT, i + 1)
                for g in range(G):
                    for n, w in enumerate((W0, W2)):
                        ins = mm(M0[:, (2 * g + n) * P:(2 * g + n + 1) * P], WT[g][:, w, :], qkT[:, g, :])
                ins.then_inc(e_qs, 1)

            def q_out(i):
                pe.wait_ge(e_gh, i + 1)
                pe.wait_ge(e_aT, i + 1)
                for g in range(G):
                    ins = mm(M1[:, g * P:(g + 1) * P], gh[:, g, :], WT[g][:, W1, :])
                ins.then_inc(e_qo, 1)

            def att_turn(i):
                pe.wait_ge(e_yT, i)
                pe.wait_ge(e_xlT, i + 1)
                pe.wait_ge(e_rawqk, i + 1)
                for n in range(4):
                    ins = pe.transpose(M1[:, n * P:(n + 1) * P], raw[:, n * P:(n + 1) * P], ident[:, :])
                ins.then_inc(e_at, 1)

            def att_scores(i, last):
                pe.wait_ge(e_aT, i + 1)
                pe.wait_ge(e_win, 2 * i + 2)
                if last:
                    pe.wait_ge(e_ur, i + 1)
                else:
                    pe.wait_ge(e_vT, i + 2)
                for h in range(NAH):
                    ins = mm(M0[:, h * 2 * P:(h + 1) * 2 * P], aqT[:, h, :], akT[:, h].rearrange("p w k -> p (w k)"))
                ins.then_inc(e_as, 1)

            def att_turn_p(i, last):
                pe.wait_ge(e_pr, i + 1)
                if last:
                    pe.wait_ge(e_to, i + 1)
                else:
                    pe.wait_ge(e_qkT, i + 2)
                for h in range(NAH):
                    for w in range(2):
                        n = 2 * h + w
                        ins = pe.transpose(M1[:, n * P:(n + 1) * P], pr[:, h, w, :], ident[:, :])
                ins.then_inc(e_ap, 1)

            def att_pv(i):
                pe.wait_ge(e_prT, i + 1)
                for h in range(NAH):
                    for w in range(2):
                        ins = mm(M0[:, h * P:(h + 1) * P], prT[:, h, w, :], vw[:, w, h * P:(h + 1) * P], w == 0, w == 1)
                ins.then_inc(e_av, 1)

            def turn_comb(i):
                pe.wait_ge(e_comb, i + 1)
                pe.wait_ge(e_prT, i + 1)
                for k in range(KT):
                    ins = pe.transpose(M1[:, k * P:(k + 1) * P], comb[:, k * P:(k + 1) * P], ident[:, :])
                ins.then_inc(e_ct, 1)

            def fc1(m):
                pe.wait_ge(e_xnT, m + 1)
                if isinstance(m, int) and m == 0:
                    pe.wait_ge(e_mmc, 1)
                else:
                    pe.wait_ge(e_combT, m)
                for k in range(KT):
                    ins = mm(M1[:, 0:P], fc1_s[:, k, :], xnT[:, k, :], k == 0, k == KT - 1)
                ins.then_inc(e_fx, 1)

            def shared_up(i, part):
                if part == 0:
                    pe.wait_ge(e_gh, i + 1)
                for c in range(part * SC // 2, (part + 1) * SC // 2):
                    for k in range(KT):
                        ins = mm(M0[:, c * P:(c + 1) * P], up_s[:, k, c * P:(c + 1) * P], xnT[:, k, :], k == 0, k == KT - 1)
                if part == 1:
                    ins.then_inc(e_upm, 1)

            def h_up(i, u):
                if u == 0:
                    pe.wait_ge(e_xlT, i + 1)
                pe.wait_ge(e_hr, NU * i + u)
                for e in range(EU):
                    ins = mm(HB[:, e * P:(e + 1) * P], e1_s[:, EU * u + e, :], xlT[:, :])
                ins.then_inc(e_h, 1)

            def y_down(i, u):
                pe.wait_ge(e_hq, NU * i + u + 1)
                pe.wait_ge(e_acc, NU * i + u)
                for e in range(EU):
                    ins = mm(YB[:, e * P:(e + 1) * P], hq[u % 2][:, e, :], e2_s[:, EU * u + e, :])
                ins.then_inc(e_y, 1)

            def turn_y(i, last):
                pe.wait_ge(e_ys, i + 1)
                if last:
                    pe.wait_ge(e_combT, i + 1)
                else:
                    pe.wait_ge(e_xlT, i + 2)
                pe.transpose(M1[:, 0:P], ys[:, :], ident[:, :]).then_inc(e_yt, 1)

            def out_down(i, part):
                if part == 0:
                    pe.wait_ge(e_comb, i + 1)
                    pe.wait_ge(e_us, i + 1)
                for c in range(part * SC // 2, (part + 1) * SC // 2):
                    mm(M0[:, 0:D], us[:, c, :], down_s[:, c, :], c == 0, False)

            def out_wo(i):
                pe.wait_ge(e_combT, i + 1)
                for k in range(KT):
                    mm(M0[:, 0:D], combT[:, k, :], wo_s[:, k, :], False, False)

            def out_fc2(i):
                pe.wait_ge(e_yT, i + 1)
                mm(M0[:, 0:D], yT[:, :], fc2_s[:, :], False, True).then_inc(e_out, 1)

            def body(i, last):
                if last:
                    q_side(i)
                    att_turn(i)
                    y_down(i, 0)
                    h_up(i, 2)
                    shared_up(i, 0)
                    shared_up(i, 1)
                    y_down(i, 1)
                    h_up(i, 3)
                    q_out(i)
                    y_down(i, 2)
                    h_up(i, 4)
                    att_scores(i, True)
                    y_down(i, 3)
                    h_up(i, 5)
                    att_turn_p(i, True)
                    y_down(i, 4)
                    h_up(i, 6)
                    att_pv(i)
                    y_down(i, 5)
                    h_up(i, 7)
                    turn_comb(i)
                    y_down(i, 6)
                    out_down(i, 0)
                    y_down(i, 7)
                    out_down(i, 1)
                    out_wo(i)
                    turn_y(i, True)
                    out_fc2(i)
                    return
                m = i + 1
                k_side(i, 0)
                k_side(i, 1)
                q_side(i)
                att_turn(i)
                y_down(i, 0)
                grads(i, 0)
                grads(i, 1)
                h_up(i, 2)
                shared_up(i, 0)
                sums(i, 0)
                sums(i, 1)
                shared_up(i, 1)
                h_up(i, 3)
                fill = {2: [lambda: q_out(i), lambda: prep_turn(m)], 3: [lambda: y_down(i, 2)],
                        4: [lambda: prep_qk(m)], 5: [lambda: prep_qk_more(m)], 6: [lambda: prep_v(m)],
                        7: [lambda: h_up(i, 5)], 8: [lambda: y_down(i, 3), lambda: prep_mom(m)],
                        9: [lambda: prep_turn_v(m), lambda: h_up(i, 6)], 10: [lambda: y_down(i, 4)],
                        11: [lambda: att_scores(i, False)], 12: [lambda: prep_turn_qk(m)],
                        13: [lambda: y_down(i, 5)], 14: [lambda: h_up(i, 7)],
                        15: [lambda: att_turn_p(i, False), lambda: y_down(i, 6)], 16: [lambda: att_pv(i)],
                        17: [lambda: y_down(i, 7)], 18: [lambda: turn_comb(i)],
                        19: [lambda: fc1(m), lambda: out_down(i, 0), lambda: out_down(i, 1)]}
                for st in range(4 * NI):
                    for g in range(G):
                        if st % 4 == 0:
                            ns_turn(g, st // 4 == NI - 1)
                            if st == 0 and g == 0:
                                y_down(i, 1)
                        elif st % 4 == 1:
                            ns_gram(g)
                            if st == 1 and g == 0:
                                h_up(i, 4)
                        elif st % 4 == 2:
                            ns_pair(g, CA, am_in, Am, Am)
                        else:
                            ns_pair(g, CB, mp_in, Mp, X)
                    for f in fill.get(st, []):
                        f()
                h_up(m, 0)
                out_wo(i)
                turn_y(i, False)
                h_up(m, 1)
                turn_w(m, 0)
                out_fc2(i)
                turn_w(m, 1)

            prep_turn(0)
            for g in range(G):
                turn_w(0, g)
            pe.wait_ge(e_const, 16 * NCONST)
            prep_qk(0)
            prep_qk_more(0)
            prep_v(0)
            prep_mom(0)
            prep_turn_v(0)
            pe.wait_ge(e_up_w, 16 * NUP)
            fc1(0)
            h_up(0, 0)
            pe.wait_ge(e_xlT, 1)
            prep_turn_qk(0)
            h_up(0, 1)
            pe.wait_ge(e_down_w, 16 * NDOWN)
            pe.wait_ge(e_later, 16 * NLATER)
            body(0, False)
            with pe.Fori(1, LAST) as i:
                body(i, False)
            body(LAST, True)

        @block.vector
        def _(dve):
            nc.vector.memset(half[:, :], 0.5)
            nc.vector.memset(neghalf[:, :], -0.5).then_inc(e_init, 1)
            nc.vector.memset(ones[:, :], 1.0)
            for it in range(NI):
                nc.vector.memset(a_tile[:, it, :], NS[it][0])
            nc.vector.memset(gs[:, NG:12], NEG)
            nc.vector.memset(akT[:, :, 1, :], 0.0)
            nc.vector.memset(vw[:, 1, :], 0.0)
            for g in range(G):
                nc.vector.memset(Mom[g][:, :, :], 0.0)
                nc.vector.memset(W1BD[g][:, :], 0.0)
                nc.vector.memset(WT[g][:, :, :], 0.0)
            nc.vector.memset(lt[:, :, :], 0.0).then_inc(e_init, 1)
            aggr_in = Expect(dve, e_stats, "aggr_in")
            rt = Expect(dve, e_rt, "route_step")

            def heads(t, n):
                return t.rearrange("p (h c) -> p h c", h=n)

            def ln_stats(m):
                dve.wait_ge(e_xa, 16 * m + 16)
                nc.vector.bn_stats(st6[:, :], xa[:, :]).then_inc(e_stats, 1)
                aggr_in.wait()
                nc.vector.bn_aggr(mv[:, :], st6[:, :]).then_inc(e_aggr, 1)
                dve.wait_ge(e_aggr, m + 1)
                nc.vector.tensor_scalar(rstd[:, 1:2], mv[:, 1:2], 1e-5, None, ALU.add).then_inc(e_veps, 1)

            def ln_norm(m):
                dve.wait_ge(e_rstd, m + 1)
                dve.wait_ge(e_pt, m)
                nc.vector.tensor_scalar(xn[:, :], xa[:, :], mv[:, 0:1], rstd[:, 0:1], ALU.subtract, ALU.mult)\
                    .then_inc(e_xn, 1)

            def prep_z(m):
                dve.wait_ge(e_rawv, m + 1)
                nc.vector.tensor_tensor(z[:, :], M1[:, D:D + SMALL], bias[:, :], ALU.add).then_inc(e_z, 1)

            def prep_silu_qk(m):
                dve.wait_ge(e_rawqk, m + 1)
                nc.vector.tensor_tensor(sl[:, 0:2 * D], raw[:, 0:2 * D], sig[:, 0:2 * D], ALU.mult).then_inc(e_slqk, 1)

            def prep_silu_v(m):
                dve.wait_ge(e_kl, m)
                dve.wait_ge(e_pnv, m)
                nc.vector.tensor_tensor(sl[:, 2 * D:3 * D], raw[:, 2 * D:3 * D], sig[:, 2 * D:3 * D], ALU.mult)\
                    .then_inc(e_slv, 1)

            def prep_ss8(m):
                dve.wait_ge(e_sq8, m + 1)
                nc.vector.tensor_reduce(r8[:, 0, :], heads(sq8[:, :], 8), AX_X, ALU.add).then_inc(e_ss8, 1)

            def prep_qkn(m):
                dve.wait_ge(e_n8, m + 1)
                nc.vector.tensor_scalar(r8[:, 2, :], r8[:, 1, :], 1e-5, None, ALU.add).then_inc(e_r8, 1)
                dve.wait_ge(e_r8, 2 * m + 1)
                nc.vector.reciprocal(r8[:, 3, :], r8[:, 2, :]).then_inc(e_r8, 1)
                dve.wait_ge(e_r8, 2 * m + 2)
                dve.wait_ge(e_pnqk, m)
                dve.wait_ge(e_kl, m)
                nc.vector.tensor_tensor(heads(qkn[:, :], 8), heads(sl[:, 0:2 * D], 8),
                                        r8[:, 3, :].unsqueeze(2).to_broadcast([P, 8, HD]), ALU.mult).then_inc(e_qkn, 1)

            def prep_mean(m):
                dve.wait_ge(e_mm, m + 1)
                for h in range(2):
                    c = slice(h * HD, (h + 1) * HD)
                    ins = nc.vector.tensor_scalar(mmc[c, :], M1[c, h:NH:2], 1.0 / P, None, ALU.mult)
                ins.then_inc(e_mmc, 1)

            def lr_a(m):
                dve.wait_ge(e_z, m + 1)
                nc.vector.scalar_tensor_tensor(lt[:, 0, :], z[:, LR:MOM], -1.0, z[:, LR:MOM], ALU.mult, ALU.min).then_inc(e_lt, 1)

            def lr_b(m):
                dve.wait_ge(e_ex, m + 1)
                nc.vector.tensor_scalar(lt[:, 2, :], lt[:, 1, :], 1.0, None, ALU.add).then_inc(e_lt, 1)
                dve.wait_ge(e_lt, 3 * m + 2)
                nc.vector.tensor_scalar(lt[:, 4, :], lt[:, 2, :], -1.0, None, ALU.add)
                nc.vector.reciprocal(lt[:, 5, :], lt[:, 2, :]).then_inc(e_lt, 1)
                dve.wait_ge(e_lt, 3 * m + 3)
                nc.vector.tensor_tensor(lt[:, 6, :], lt[:, 1, :], lt[:, 4, :], ALU.subtract).then_inc(e_lr_steps, 1)
                dve.wait_ge(e_lr_steps, 3 * m + 1)
                nc.vector.tensor_tensor(lt[:, 6, :], lt[:, 6, :], lt[:, 5, :], ALU.mult).then_inc(e_lr_steps, 1)

            def lr_c(m):
                dve.wait_ge(e_ln, m + 1)
                nc.vector.scalar_tensor_tensor(lt[:, 7, :], z[:, LR:MOM], 0.0, lt[:, 3, :], ALU.max, ALU.add)\
                    .then_inc(e_lr_steps, 1)
                dve.wait_ge(e_lr_steps, 3 * m + 3)
                dve.wait_ge(e_kl, m)
                nc.vector.tensor_tensor(lr[:, :, :].rearrange("p h n -> p (h n)"), lt[:, 7, :], lt[:, 6, :], ALU.add)\
                    .then_inc(e_lr, 1)

            def k_side(i):
                tt, stt = nc.vector.tensor_tensor, nc.vector.scalar_tensor_tensor
                sg, hbm, dhi = ([ks[g][:, n, :] for g in range(G)] for n in range(3))

                def silu(g):
                    dve.wait_ge(e_kc[g], i + 1)
                    tt(kt[g][:, 0, :], CB[g][:, 0:P], sg[g], ALU.mult).then_inc(e_kd[g], 1)

                def slope(g):
                    dve.wait_ge(e_kd[g], 3 * i + 1)
                    stt(kt[g][:, 1, :], sg[g], 1.0, kt[g][:, 0, :], ALU.subtract, ALU.mult).then_inc(e_kd[g], 1)

                def derivative(g):
                    dve.wait_ge(e_kd[g], 3 * i + 2)
                    tt(kt[g][:, 2, :], sg[g], kt[g][:, 1, :], ALU.subtract).then_inc(e_kd[g], 1)

                def through(g):
                    dve.wait_ge(e_kd[g], 3 * i + 3)
                    dve.wait_ge(e_ku[g], i + 1)
                    tt(dga[g][:, :], kt[g][:, 2, :], kt[g][:, 3, :], ALU.mult).then_inc(e_dgr[g], 1)

                def hidden(g):
                    tt(hid[g][:, :], kt[g][:, 0, :], hbm[g], ALU.mult)

                def dhidden(g):
                    tt(dhb[g][:, :], kt[g][:, 0, :], dhi[g], ALU.mult)

                for step, g in ((silu, 0), (slope, 0), (hidden, 0), (silu, 1), (derivative, 0), (dhidden, 0), (slope, 1),
                                (through, 0), (hidden, 1), (derivative, 1), (dhidden, 1), (through, 1)):
                    step(g)

            def grad(i):
                flat = "p w c -> p (w c)"
                for g in range(G):
                    dve.wait_ge(e_dw[g], i + 1)
                    nc.vector.scalar_tensor_tensor(Mom[g][:, :, :].rearrange(flat), Mom[g][:, :, :].rearrange(flat),
                                                   mmc[:, g:g + 1], CA[g][:, 0:3 * HD], ALU.mult, ALU.add).then_inc(e_G[g], 1)
                for g in range(G):
                    dve.wait_ge(e_G[g], i + 1)
                    nc.vector.tensor_tensor(sq3[g][:, :, :], Mom[g][:, :, :], Mom[g][:, :, :], ALU.mult).then_inc(e_s3[g], 1)
                for g in range(G):
                    dve.wait_ge(e_s3[g], 2 * i + 1)
                    nc.vector.tensor_reduce(r3[g][:, 0, :], sq3[g][:, :, :], AX_X, ALU.add).then_inc(e_s3[g], 1)

            def sum_copy(i, g):
                dve.wait_ge(e_ssb[g], i + 1)
                nc.vector.tensor_copy(r3[g][:, 1, :], CB[g][:, 0:3]).then_inc(e_sst[g], 1)

            def x_first(i):
                for g in range(G):
                    dve.wait_ge(e_pw[g], i + 1)
                    nc.vector.tensor_scalar(r3[g][:, 2, :], r3[g][:, 2, :], 1e-7, None, ALU.add).then_inc(e_sst[g], 1)
                    dve.wait_ge(e_sst[g], 3 * i + 2)
                    nc.vector.reciprocal(r3[g][:, 1, :], r3[g][:, 2, :]).then_inc(e_sst[g], 1)
                    dve.wait_ge(e_sst[g], 3 * i + 3)
                    nc.vector.tensor_tensor(X[g][:, :, :], Mom[g][:, :, :],
                                            r3[g][:, 1, :].unsqueeze(2).to_broadcast([P, 3, HD]), ALU.mult).then_inc(e_x[g], 1)

            def ns_a(i, g, it):
                dve.wait_ge(e_prod[g], 3 * NI * i + 3 * it + 1)
                nc.vector.tensor_copy(Am[g][:, :, :].rearrange("p w c -> p (w c)"), CB[g][:, 0:3 * HD]).then_inc(e_am[g], 1)

            def ns_m(i, g, it):
                _, b, c = NS[it]
                dve.wait_ge(e_prod[g], 3 * NI * i + 3 * it + 2)
                nc.vector.scalar_tensor_tensor(Mp[g][:, :, :].rearrange("p w c -> p (w c)"),
                                               Am[g][:, :, :].rearrange("p w c -> p (w c)"), b / c, CA[g][:, 0:3 * HD],
                                               ALU.mult, ALU.add).then_inc(e_mp[g], 1)

            def ns_x(i, g, it):
                dve.wait_ge(e_prod[g], 3 * NI * i + 3 * it + 3)
                dve.wait_ge(e_ax[g], NI * i + it + 1)
                nc.vector.scalar_tensor_tensor(X[g][:, :, :].rearrange("p w c -> p (w c)"), CB[g][:, 0:3 * HD], NS[it][2],
                                               aX[g][:, :, :].rearrange("p w c -> p (w c)"), ALU.mult, ALU.add)\
                    .then_inc(e_x[g], 1)

            def row_sums(m):
                for g in range(G):
                    nc.vector.tensor_tensor(sq3[g][:, :, :], Wn[g][:, :, :], Wn[g][:, :, :], ALU.mult).then_inc(e_up[g], 1)
                for g in range(G):
                    dve.wait_ge(e_up[g], 4 * m + 1)
                    nc.vector.tensor_reduce(r3[g][:, 3, :], sq3[g][:, :, :], AX_X, ALU.add).then_inc(e_rn[g], 1)

            def update(i):
                for g in range(G):
                    dve.wait_ge(e_x[g], (NI + 1) * i + NI + 1)
                    nc.vector.tensor_tensor(Wn[g][:, :, :], Wn[g][:, :, :], X[g][:, :, :], ALU.add).then_inc(e_up[g], 1)
                for g in range(G):
                    dve.wait_ge(e_up[g], 4 * i + 4)
                row_sums(i + 1)

            def renorm(m):
                for g in range(G):
                    dve.wait_ge(e_rp[g], m + 1)
                    nc.vector.tensor_scalar(r3[g][:, 4, :], r3[g][:, 4, :], 1e-5, None, ALU.add).then_inc(e_up[g], 1)
                    dve.wait_ge(e_up[g], 4 * m + 2)
                    nc.vector.reciprocal(r3[g][:, 5, :], r3[g][:, 4, :]).then_inc(e_up[g], 1)
                    dve.wait_ge(e_up[g], 4 * m + 3)
                    for w in range(3):
                        ins = nc.vector.tensor_scalar(Wn[g][:, w, :], Wn[g][:, w, :], r3[g][:, 5, w:w + 1],
                                                      nrm[g][:, w:w + 1], ALU.mult, ALU.mult)
                    ins.then_inc(e_wn[g], 1)

            def w_bd(m):
                for g in range(G):
                    if isinstance(m, int) and m == 0:
                        dve.wait_ge(e_ttw, 16 * G)
                    else:
                        dve.wait_ge(e_wn[g], m)
                    nc.vector.tensor_copy(W1BD[g][0:HD, 0:HD], Wn[g][0:HD, W1, :])
                    nc.vector.tensor_copy(W1BD[g][HD:P, HD:P], Wn[g][HD:P, W1, :]).then_inc(e_bd[g], 1)

            def q_gate(i):
                dve.wait_ge(e_gsig, i + 1)
                v = M0[:, :].rearrange("p (g w t) -> p g w t", g=G, w=2)
                nc.vector.tensor_tensor(gt1[:, :, :], v[:, :, 0, :], gsig[:, :, :], ALU.mult).then_inc(e_gt1, 1)
                dve.wait_ge(e_gt1, i + 1)
                nc.vector.tensor_tensor(gh[:, :, :], v[:, :, 1, :], gt1[:, :, :], ALU.mult).then_inc(e_gh, 1)

            def q_ms(i):
                dve.wait_ge(e_to, i + 1)
                nc.vector.tensor_reduce(r4[:, 0, :], heads(tsq[:, :], NH), AX_X, ALU.add).then_inc(e_msq, 1)
                dve.wait_ge(e_msq, 2 * i + 1)
                nc.vector.tensor_scalar(r4[:, 0, :], r4[:, 0, :], 1.0 / HD, 1e-5, ALU.mult, ALU.add).then_inc(e_msq, 1)

            def q_norm(i):
                nc.vector.tensor_tensor(r4[:, 2, :], z[:, SCL:GATE], sgs[:, SCL - MOM:GATE - MOM], ALU.mult).then_inc(e_tf, 1)
                dve.wait_ge(e_tf, 3 * i + 1)
                dve.wait_ge(e_rms, i + 1)
                nc.vector.tensor_tensor(r4[:, 3, :], r4[:, 2, :], r4[:, 1, :], ALU.mult).then_inc(e_tf, 1)
                dve.wait_ge(e_tf, 3 * i + 2)
                nc.vector.tensor_tensor(heads(tt1[:, :], NH), heads(to[:, :], NH),
                                        r4[:, 3, :].unsqueeze(2).to_broadcast([P, NH, HD]), ALU.mult).then_inc(e_tf, 1)
                dve.wait_ge(e_tf, 3 * i + 3)
                nc.vector.tensor_tensor(heads(ttt[:, :], NH), heads(tt1[:, :], NH),
                                        og_s[:, :].unsqueeze(1).to_broadcast([P, NH, HD]), ALU.mult).then_inc(e_ttt, 1)

            def att_scale(i):
                dve.wait_ge(e_at, i + 1)
                dve.wait_ge(e_win, 2 * i + 1)
                for c, dst in ((0, [aqT[:, h, :] for h in range(NAH)]), (1, [akT[:, h, 1, :] for h in range(NAH)])):
                    for h in range(NAH):
                        n = 2 * c + h
                        ins = nc.vector.tensor_scalar(dst[h], M1[:, n * P:(n + 1) * P], affine[:, h, c:c + 1],
                                                      affine[:, h, 2 + c:3 + c], ALU.mult, ALU.add)
                ins.then_inc(e_aT, 1)

            def att_mask(i):
                dve.wait_ge(e_as, i + 1)
                if not (isinstance(i, int) and i == 0):
                    dve.wait_ge(e_mask, 1)
                nc.vector.tensor_tensor(sm[:, :, :, :].rearrange("p h w k -> p h (w k)"), heads(M0[:, :], NAH),
                                        mask[:, :, :].rearrange("p w k -> p (w k)").unsqueeze(1)
                                        .to_broadcast([P, NAH, 2 * P]), ALU.add).then_inc(e_sm, 1)

            def att_max(i):
                dve.wait_ge(e_sm, i + 1)
                nc.vector.tensor_reduce(r2[:, 0, :], sm[:, :, :, :].rearrange("p h w k -> p h (w k)"), AX_X, ALU.max)\
                    .then_inc(e_nmx, 1)
                dve.wait_ge(e_nmx, i + 1)
                nc.vector.tensor_scalar(r2[:, 1, :], r2[:, 0, :], -ATT_SCALE, None, ALU.mult).then_inc(e_nb, 1)

            def att_out(i):
                nc.vector.wait_ge(e_pr, i + 1)
                nc.vector.reciprocal(r2[:, 3, :], r2[:, 2, :]).then_inc(e_at2, 1)
                dve.wait_ge(e_at2, 2 * i + 1)
                dve.wait_ge(e_av, i + 1)
                nc.vector.tensor_tensor(heads(att[:, :], NAH), heads(M0[:, 0:D], NAH),
                                        r2[:, 3, :].unsqueeze(2).to_broadcast([P, NAH, P]), ALU.mult).then_inc(e_at2, 1)
                dve.wait_ge(e_at2, 2 * i + 2)
                dve.wait_ge(e_ttt, i + 1)
                nc.vector.tensor_tensor(comb[:, :], att[:, :], ttt[:, :], ALU.add).then_inc(e_comb, 1)

            def route(m):
                scores = sgs[:, GATE - MOM:SMALL - MOM]

                def biased():
                    dve.wait_ge(e_sgs, m + 1)
                    return nc.vector.tensor_tensor(sbias[:, :], scores, gb[:, :], ALU.add)

                def group_best():
                    for n in range(NG):
                        ins = nc.vector.max(g8[:, n, :], sbias[:, n * EPG:(n + 1) * EPG])
                    return ins

                def group_sum():
                    return nc.vector.tensor_tensor(gs[:, 0:NG], g8[:, :, 0], g8[:, :, 1], ALU.add)

                def groups_sorted():
                    return nc.vector.max(t8[:, :], gs[:, :])

                def groups_two():
                    return nc.vector.memset(t8[:, 2:8], NEG)

                def groups_marked():
                    return nc.vector.match_replace(gm[:, :], t8[:, :], gs[:, :], TAKEN)

                def penalty():
                    return nc.vector.tensor_scalar(pen[:, :], gm[:, 0:NG], TAKEN, 1.0, ALU.is_equal, ALU.subtract)

                def masked():
                    return nc.vector.scalar_tensor_tensor(
                        heads(msk[:, :], NG), pen[:, :].unsqueeze(2).to_broadcast([P, NG, EPG]), -NEG,
                        heads(sbias[:, :], NG), ALU.mult, ALU.add)

                def best():
                    return nc.vector.max(m8[:, :], msk[:, :])

                def best_marked():
                    return nc.vector.match_replace(mr[:, :], m8[:, :], msk[:, :], TAKEN)

                def selected():
                    return nc.vector.scalar_tensor_tensor(csel[:, :], mr[:, :], TAKEN, scores, ALU.is_equal, ALU.mult)

                def selected_sum():
                    return nc.vector.tensor_reduce(cs1[:, 0:1], csel[:, :], AX_X, ALU.add)

                def inverse():
                    return nc.vector.reciprocal(cs1[:, 1:2], cs1[:, 0:1])

                def after(step):
                    def run():
                        rt.wait()
                        step().then_inc(e_rt, 1)
                    return run

                rest = (group_best, group_sum, groups_sorted, groups_two, groups_marked, penalty, masked, best,
                        best_marked, selected, selected_sum, inverse)
                return [lambda: biased().then_inc(e_rt, 1)] + [after(step) for step in rest]

            def weights(m):
                rt.wait()
                dve.wait_ge(e_acc, NU * m)
                nc.vector.tensor_scalar(cw[:, :], csel[:, :], cs1[:, 1:2], ROUTED_SCALE, ALU.mult, ALU.mult).then_inc(e_cw, 1)

            def y_acc(i, u):
                dve.wait_ge(e_y, NU * i + u + 1)
                dve.wait_ge(e_acc, NU * i + u)
                for e in range(EU):
                    w = cw[:, EU * u + e:EU * u + e + 1]
                    y = YB[:, e * P:(e + 1) * P]
                    ins = nc.vector.scalar_tensor_tensor(acc[:, e, :], y, w, acc[:, e, :], ALU.mult, ALU.add)
                ins.then_inc(e_acc, 1)

            def y_sum(i):
                dve.wait_ge(e_acc, NU * i + NU)
                nc.vector.tensor_tensor(ya[:, :, :], acc[:, 0:2, :], acc[:, 2:4, :], ALU.add).then_inc(e_ya, 1)
                dve.wait_ge(e_ya, i + 1)
                nc.vector.tensor_tensor(ys[:, :], ya[:, 0, :], ya[:, 1, :], ALU.add).then_inc(e_ys, 1)

            def total(i):
                dve.wait_ge(e_out, i + 1)
                dve.wait_ge(e_xr, 16 * i + 16)
                dve.wait_ge(e_stored, 16 * i)
                nc.vector.tensor_tensor(ot[:, :], M0[:, 0:D], xr[:, :], ALU.add).then_inc(e_ot, 1)

            def body(i, last):
                if last:
                    q_gate(i)
                    att_scale(i)
                    y_acc(i, 1)
                    q_ms(i)
                    y_acc(i, 2)
                    att_mask(i)
                    att_max(i)
                    y_acc(i, 3)
                    q_norm(i)
                    y_acc(i, 4)
                    att_out(i)
                    for u in range(5, NU):
                        y_acc(i, u)
                    y_sum(i)
                    total(i)
                    return
                m = i + 1
                ln_stats(m)
                k_side(i)
                q_gate(i)
                grad(i)
                sum_copy(i, 0)
                sum_copy(i, 1)
                x_first(i)
                routing = route(m)
                fill = {0: [lambda: ln_norm(m), lambda: att_scale(i)], 2: [lambda: y_acc(i, 1)],
                        3: [lambda: q_ms(i)], 4: [lambda: y_acc(i, 2)],
                        5: [lambda: q_norm(i)], 7: [lambda: prep_silu_qk(m), lambda: prep_z(m)],
                        8: [lambda: prep_silu_v(m), lambda: prep_ss8(m)], 9: [lambda: y_acc(i, 3), lambda: prep_mean(m)],
                        10: [lambda: lr_a(m), lambda: prep_qkn(m)],
                        11: [lambda: y_acc(i, 4)], 12: [lambda: att_mask(i)], 13: [lambda: att_max(i), lambda: y_acc(i, 5)],
                        14: [lambda: lr_b(m)], 15: [lambda: y_acc(i, 6)], 16: [lambda: lr_c(m)],
                        17: [lambda: att_out(i)], 18: [lambda: y_acc(i, 7)]}
                for st in range(4 * NI):
                    for g in range(G):
                        if st % 4:
                            (ns_a, ns_m, ns_x)[st % 4 - 1](i, g, st // 4)
                        if st > 10 and routing:
                            routing.pop(0)()
                    for f in fill.get(st, []):
                        f()
                update(i)
                y_sum(i)
                renorm(m)
                w_bd(m)
                total(i)
                weights(m)

            dve.wait_ge(e_init, 2)
            ln_stats(0)
            ln_norm(0)
            dve.wait_ge(e_ttw, 16 * G)
            row_sums(0)
            for g in range(G):
                dve.wait_ge(e_rp[g], 1)
                nc.vector.tensor_copy(nrm[g][:, :], r3[g][:, 4, :]).then_inc(e_up[g], 2)
            w_bd(0)
            dve.wait_ge(e_const, 16 * NCONST)
            prep_z(0)
            prep_silu_qk(0)
            prep_silu_v(0)
            routing = route(0)
            between = {0: lambda: prep_ss8(0), 1: lambda: lr_a(0), 2: lambda: prep_mean(0), 5: lambda: prep_qkn(0),
                       6: lambda: lr_b(0), 9: lambda: lr_c(0)}
            for n, step in enumerate(routing):
                step()
                if n in between:
                    between[n]()
            weights(0)
            dve.wait_ge(e_later, 16 * NLATER)
            body(0, False)
            with dve.Fori(1, LAST) as i:
                body(i, False)
            body(LAST, True)


def kernel(**inputs):
    import numpy as np
    import concourse.bacc as bacc
    from concourse.bass_utils import run_bass_kernel_spmd as run

    a = {k.replace("L0_", ""): np.asarray(v) for k, v in inputs.items()}
    q, k = np.arange(P)[:, None], np.arange(P)[None, :]
    block = np.kron(np.eye(2), np.ones((HD, HD)))
    fixed = np.stack([block, np.full((P, P), NEG), np.where(k <= q, 0.0, NEG), np.where(k >= q, 0.0, NEG)], 1)
    wall = np.concatenate([a["attn_Wqkv"], a["attn_Wlr"], a["attn_Wm"], a["attn_Ws"], a["ffn_gate_w"].T], 1)
    rows = np.concatenate([np.full(MOM - LR, LR_INV, np.float32), a["attn_bm"], a["attn_bs"],
                           np.zeros(SMALL - GATE, np.float32), a["ffn_gate_bias"], a["attn_o_norm_g"]])
    fast = np.stack([a[n].reshape(G, P, HD) for n in ("attn_w0", "attn_w2", "attn_w1")], 2)
    affine = np.concatenate([a["attn_qk_scale"], a["attn_qk_offset"]], 1)
    arrays = {
        "x": a["attn_x"].reshape(-1, D), "wall": wall.reshape(KT, P, -1).transpose(1, 0, 2), "rows": rows,
        "wo": a["attn_Wo"], "fast": fast, "affine": affine.reshape(NAH, AHD, 4).transpose(1, 0, 2),
        "fc1T": a["ffn_fc1_w"].T, "fc2T": a["ffn_fc2_w"].T,
        "e1T": a["ffn_w1"].transpose(2, 0, 1), "e2T": a["ffn_w2"].transpose(2, 0, 1),
        "upT": a["ffn_shared_up_w"].T, "downT": a["ffn_shared_down_w"].T,
        "ident": np.eye(P, dtype=np.float32), "fixed": fixed.astype(np.float32),
    }
    arrays = {f"in_{n}": np.ascontiguousarray(v) for n, v in arrays.items()}
    nc = bacc.Bacc("TRN2", target_bir_lowering=False, num_devices=1)
    args = [nc.dram_tensor(n, v.shape, mybir.dt.from_np(v.dtype), kind="ExternalInput").ap() for n, v in arrays.items()]
    shape = arrays["in_x"].shape
    build(nc, *args, nc.dram_tensor("out_0", shape, F32, kind="ExternalOutput").ap())
    r = run(nc, [arrays], core_ids=[0])
    return r.results[0]["out_0"].reshape(1, *shape)
```
